# Optimizing a Trainium2 kernel written in Bass

```python
import numpy as np
import jax
import jax.numpy as jnp

def _softmax(x, axis=-1):
    return jax.nn.softmax(x, axis=axis)

def _gelu(x):
    return jax.nn.gelu(x, approximate=True)

def _silu(x):
    return jax.nn.silu(x)

def _sigmoid(x):
    return jax.nn.sigmoid(x)

def _layernorm(x, axis=-1, eps=1e-05):
    m = jnp.mean(x, axis=axis, keepdims=True)
    v = jnp.var(x, axis=axis, keepdims=True)
    return (x - m) / jnp.sqrt(v + eps)

def _scatter_add(tgt, idx, src, axis=0):
    return tgt.at[idx].add(src)

def _segment_sum(src, seg, n):
    return jax.ops.segment_sum(src, seg, n)
kernel_name = 'mk_dlrm_tower_d1_rec_r8_e5a876'

def setup_inputs(seed: int=0):
    np.random.seed(seed)
    _w = jnp.asarray

    def _rec_inputs():
        import jax
        import jax.numpy as jnp
        _tk = jax.random.key(seed)
        dense_ctx = jax.random.normal(jax.random.fold_in(_tk, 190), (512, 16), jnp.float32)
        ids = jnp.stack([jax.random.randint(jax.random.fold_in(_tk, 200 + f), (512,), 0, v, jnp.int32) for f, v in enumerate([1000, 12500, 125000, 125000, 1250, 125000, 12500, 1000, 125000, 12500, 1000, 12500, 125000, 12500, 1000, 1250, 1250, 1250, 125000, 1250, 12500, 1000, 12500, 12500, 1250, 125000, 12500, 125000, 12500, 125000, 1000, 1000, 1250, 1250, 1000, 125000, 125000, 1250, 1250, 125000])], axis=1)
        tbl_0 = 0.05 * jax.random.normal(jax.random.fold_in(_tk, 500 + 0), (1000, 16), jnp.float32)
        tbl_1 = 0.05 * jax.random.normal(jax.random.fold_in(_tk, 500 + 1), (12500, 16), jnp.float32)
        tbl_2 = 0.05 * jax.random.normal(jax.random.fold_in(_tk, 500 + 2), (125000, 16), jnp.float32)
        tbl_3 = 0.05 * jax.random.normal(jax.random.fold_in(_tk, 500 + 3), (125000, 16), jnp.float32)
        tbl_4 = 0.05 * jax.random.normal(jax.random.fold_in(_tk, 500 + 4), (1250, 16), jnp.float32)
        tbl_5 = 0.05 * jax.random.normal(jax.random.fold_in(_tk, 500 + 5), (125000, 16), jnp.float32)
        tbl_6 = 0.05 * jax.random.normal(jax.random.fold_in(_tk, 500 + 6), (12500, 16), jnp.float32)
        tbl_7 = 0.05 * jax.random.normal(jax.random.fold_in(_tk, 500 + 7), (1000, 16), jnp.float32)
        tbl_8 = 0.05 * jax.random.normal(jax.random.fold_in(_tk, 500 + 8), (125000, 16), jnp.float32)
        tbl_9 = 0.05 * jax.random.normal(jax.random.fold_in(_tk, 500 + 9), (12500, 16), jnp.float32)
        tbl_10 = 0.05 * jax.random.normal(jax.random.fold_in(_tk, 500 + 10), (1000, 16), jnp.float32)
        tbl_11 = 0.05 * jax.random.normal(jax.random.fold_in(_tk, 500 + 11), (12500, 16), jnp.float32)
        tbl_12 = 0.05 * jax.random.normal(jax.random.fold_in(_tk, 500 + 12), (125000, 16), jnp.float32)
        tbl_13 = 0.05 * jax.random.normal(jax.random.fold_in(_tk, 500 + 13), (12500, 16), jnp.float32)
        tbl_14 = 0.05 * jax.random.normal(jax.random.fold_in(_tk, 500 + 14), (1000, 16), jnp.float32)
        tbl_15 = 0.05 * jax.random.normal(jax.random.fold_in(_tk, 500 + 15), (1250, 16), jnp.float32)
        tbl_16 = 0.05 * jax.random.normal(jax.random.fold_in(_tk, 500 + 16), (1250, 16), jnp.float32)
        tbl_17 = 0.05 * jax.random.normal(jax.random.fold_in(_tk, 500 + 17), (1250, 16), jnp.float32)
        tbl_18 = 0.05 * jax.random.normal(jax.random.fold_in(_tk, 500 + 18), (125000, 16), jnp.float32)
        tbl_19 = 0.05 * jax.random.normal(jax.random.fold_in(_tk, 500 + 19), (1250, 16), jnp.float32)
        tbl_20 = 0.05 * jax.random.normal(jax.random.fold_in(_tk, 500 + 20), (12500, 16), jnp.float32)
        tbl_21 = 0.05 * jax.random.normal(jax.random.fold_in(_tk, 500 + 21), (1000, 16), jnp.float32)
        tbl_22 = 0.05 * jax.random.normal(jax.random.fold_in(_tk, 500 + 22), (12500, 16), jnp.float32)
        tbl_23 = 0.05 * jax.random.normal(jax.random.fold_in(_tk, 500 + 23), (12500, 16), jnp.float32)
        tbl_24 = 0.05 * jax.random.normal(jax.random.fold_in(_tk, 500 + 24), (1250, 16), jnp.float32)
        tbl_25 = 0.05 * jax.random.normal(jax.random.fold_in(_tk, 500 + 25), (125000, 16), jnp.float32)
        tbl_26 = 0.05 * jax.random.normal(jax.random.fold_in(_tk, 500 + 26), (12500, 16), jnp.float32)
        tbl_27 = 0.05 * jax.random.normal(jax.random.fold_in(_tk, 500 + 27), (125000, 16), jnp.float32)
        tbl_28 = 0.05 * jax.random.normal(jax.random.fold_in(_tk, 500 + 28), (12500, 16), jnp.float32)
        tbl_29 = 0.05 * jax.random.normal(jax.random.fold_in(_tk, 500 + 29), (125000, 16), jnp.float32)
        tbl_30 = 0.05 * jax.random.normal(jax.random.fold_in(_tk, 500 + 30), (1000, 16), jnp.float32)
        tbl_31 = 0.05 * jax.random.normal(jax.random.fold_in(_tk, 500 + 31), (1000, 16), jnp.float32)
        tbl_32 = 0.05 * jax.random.normal(jax.random.fold_in(_tk, 500 + 32), (1250, 16), jnp.float32)
        tbl_33 = 0.05 * jax.random.normal(jax.random.fold_in(_tk, 500 + 33), (1250, 16), jnp.float32)
        tbl_34 = 0.05 * jax.random.normal(jax.random.fold_in(_tk, 500 + 34), (1000, 16), jnp.float32)
        tbl_35 = 0.05 * jax.random.normal(jax.random.fold_in(_tk, 500 + 35), (125000, 16), jnp.float32)
        tbl_36 = 0.05 * jax.random.normal(jax.random.fold_in(_tk, 500 + 36), (125000, 16), jnp.float32)
        tbl_37 = 0.05 * jax.random.normal(jax.random.fold_in(_tk, 500 + 37), (1250, 16), jnp.float32)
        tbl_38 = 0.05 * jax.random.normal(jax.random.fold_in(_tk, 500 + 38), (1250, 16), jnp.float32)
        tbl_39 = 0.05 * jax.random.normal(jax.random.fold_in(_tk, 500 + 39), (125000, 16), jnp.float32)
        _rk = jax.random.fold_in(_tk, 7)
        W_top1 = 0.05 * jax.random.normal(jax.random.fold_in(_tk, 801), (400, 512), jnp.float32)
        W_top2 = 0.0441942 * jax.random.normal(jax.random.fold_in(_tk, 802), (512, 256), jnp.float32)
        W_top3 = 0.0625 * jax.random.normal(jax.random.fold_in(_tk, 803), (256, 1), jnp.float32)
        b_top1 = jnp.zeros((512,), jnp.float32)
        b_top2 = jnp.zeros((256,), jnp.float32)
        return (dense_ctx, ids, tbl_0, tbl_1, tbl_2, tbl_3, tbl_4, tbl_5, tbl_6, tbl_7, tbl_8, tbl_9, tbl_10, tbl_11, tbl_12, tbl_13, tbl_14, tbl_15, tbl_16, tbl_17, tbl_18, tbl_19, tbl_20, tbl_21, tbl_22, tbl_23, tbl_24, tbl_25, tbl_26, tbl_27, tbl_28, tbl_29, tbl_30, tbl_31, tbl_32, tbl_33, tbl_34, tbl_35, tbl_36, tbl_37, tbl_38, tbl_39, W_top1, b_top1, W_top2, b_top2, W_top3)
    dense_ctx, ids, tbl_0, tbl_1, tbl_2, tbl_3, tbl_4, tbl_5, tbl_6, tbl_7, tbl_8, tbl_9, tbl_10, tbl_11, tbl_12, tbl_13, tbl_14, tbl_15, tbl_16, tbl_17, tbl_18, tbl_19, tbl_20, tbl_21, tbl_22, tbl_23, tbl_24, tbl_25, tbl_26, tbl_27, tbl_28, tbl_29, tbl_30, tbl_31, tbl_32, tbl_33, tbl_34, tbl_35, tbl_36, tbl_37, tbl_38, tbl_39, W_top1, b_top1, W_top2, b_top2, W_top3 = _rec_inputs()

    def _L0_rec_setup():
        import jax, jax.numpy as jnp
        import numpy as np
        B, M, D = (512, 40, 16)
        DIMS = [128, 128, 128]
        key = jax.random.key(seed)
        k_x, k0, k1, k2 = jax.random.split(key, 4)
        scale = lambda fan_in: (2.0 / fan_in) ** 0.5
        x0 = jax.random.normal(k_x, (B, M, D), dtype=jnp.float32)
        kern0 = jax.random.normal(k0, (DIMS[0], M, M), dtype=jnp.float32) * scale(M * M)
        kern1 = jax.random.normal(k1, (DIMS[1], DIMS[0], M), dtype=jnp.float32) * scale(DIMS[0] * M)
        kern2 = jax.random.normal(k2, (DIMS[2], DIMS[1], M), dtype=jnp.float32) * scale(DIMS[1] * M)
        return {'x0': x0, 'k0': kern0, 'k1': kern1, 'k2': kern2}
    _L0_rec_all = _L0_rec_setup()
    _L0_rec_in = {k: v for k, v in _L0_rec_all.items() if k in ('k0', 'k1', 'k2')}
    del _L0_rec_all
    return {'dense_ctx': dense_ctx, 'ids': ids, 'tbl_0': tbl_0, 'tbl_1': tbl_1, 'tbl_2': tbl_2, 'tbl_3': tbl_3, 'tbl_4': tbl_4, 'tbl_5': tbl_5, 'tbl_6': tbl_6, 'tbl_7': tbl_7, 'tbl_8': tbl_8, 'tbl_9': tbl_9, 'tbl_10': tbl_10, 'tbl_11': tbl_11, 'tbl_12': tbl_12, 'tbl_13': tbl_13, 'tbl_14': tbl_14, 'tbl_15': tbl_15, 'tbl_16': tbl_16, 'tbl_17': tbl_17, 'tbl_18': tbl_18, 'tbl_19': tbl_19, 'tbl_20': tbl_20, 'tbl_21': tbl_21, 'tbl_22': tbl_22, 'tbl_23': tbl_23, 'tbl_24': tbl_24, 'tbl_25': tbl_25, 'tbl_26': tbl_26, 'tbl_27': tbl_27, 'tbl_28': tbl_28, 'tbl_29': tbl_29, 'tbl_30': tbl_30, 'tbl_31': tbl_31, 'tbl_32': tbl_32, 'tbl_33': tbl_33, 'tbl_34': tbl_34, 'tbl_35': tbl_35, 'tbl_36': tbl_36, 'tbl_37': tbl_37, 'tbl_38': tbl_38, 'tbl_39': tbl_39, 'W_top1': W_top1, 'b_top1': b_top1, 'W_top2': W_top2, 'b_top2': b_top2, 'W_top3': W_top3, 'L0_rec_k0': _L0_rec_in['k0'], 'L0_rec_k1': _L0_rec_in['k1'], 'L0_rec_k2': _L0_rec_in['k2']}

def reference(dense_ctx, ids, tbl_0, tbl_1, tbl_2, tbl_3, tbl_4, tbl_5, tbl_6, tbl_7, tbl_8, tbl_9, tbl_10, tbl_11, tbl_12, tbl_13, tbl_14, tbl_15, tbl_16, tbl_17, tbl_18, tbl_19, tbl_20, tbl_21, tbl_22, tbl_23, tbl_24, tbl_25, tbl_26, tbl_27, tbl_28, tbl_29, tbl_30, tbl_31, tbl_32, tbl_33, tbl_34, tbl_35, tbl_36, tbl_37, tbl_38, tbl_39, W_top1, b_top1, W_top2, b_top2, W_top3, L0_rec_k0, L0_rec_k1, L0_rec_k2):
    import jax
    import jax.numpy as jnp

    def _L0_rec_ref(x0, k0, k1, k2):
        import jax, jax.numpy as jnp
        import numpy as np
        B, M, D = (512, 40, 16)
        DIMS = [128, 128, 128]
        x = x0
        outputs = []
        for k in (k0, k1, k2):
            x = jnp.einsum('bhd,bmd,ohm->bod', x, x0, k)
            outputs.append(jnp.sum(x, axis=-1))
        return jnp.concatenate(outputs, axis=1)
    e = jnp.stack([tbl_0[ids[:, 0]], tbl_1[ids[:, 1]], tbl_2[ids[:, 2]], tbl_3[ids[:, 3]], tbl_4[ids[:, 4]], tbl_5[ids[:, 5]], tbl_6[ids[:, 6]], tbl_7[ids[:, 7]], tbl_8[ids[:, 8]], tbl_9[ids[:, 9]], tbl_10[ids[:, 10]], tbl_11[ids[:, 11]], tbl_12[ids[:, 12]], tbl_13[ids[:, 13]], tbl_14[ids[:, 14]], tbl_15[ids[:, 15]], tbl_16[ids[:, 16]], tbl_17[ids[:, 17]], tbl_18[ids[:, 18]], tbl_19[ids[:, 19]], tbl_20[ids[:, 20]], tbl_21[ids[:, 21]], tbl_22[ids[:, 22]], tbl_23[ids[:, 23]], tbl_24[ids[:, 24]], tbl_25[ids[:, 25]], tbl_26[ids[:, 26]], tbl_27[ids[:, 27]], tbl_28[ids[:, 28]], tbl_29[ids[:, 29]], tbl_30[ids[:, 30]], tbl_31[ids[:, 31]], tbl_32[ids[:, 32]], tbl_33[ids[:, 33]], tbl_34[ids[:, 34]], tbl_35[ids[:, 35]], tbl_36[ids[:, 36]], tbl_37[ids[:, 37]], tbl_38[ids[:, 38]], tbl_39[ids[:, 39]]], axis=1)
    z = _L0_rec_ref(e, L0_rec_k0, L0_rec_k1, L0_rec_k2)
    z = z.reshape(z.shape[0], -1)
    h = jnp.concatenate([z, dense_ctx], axis=1)
    h = jnp.maximum(h @ W_top1 + b_top1, 0.0)
    h = jnp.maximum(h @ W_top2 + b_top2, 0.0)
    y = h @ W_top3
    return y

_drawn_inputs = setup_inputs


def setup_inputs(seed=0):
    import zlib

    import numpy as np

    out = dict(_drawn_inputs(seed))
    spreads = {'b_top1': (0.0, 0.524), 'b_top2': (0.0, 0.1)}
    factors = {'tbl_0': 7.837,
     'tbl_1': 7.185,
     'tbl_2': 6.762,
     'tbl_3': 7.25,
     'tbl_4': 6.887,
     'tbl_5': 7.402,
     'tbl_6': 7.047,
     'tbl_7': 7.488,
     'tbl_8': 6.845,
     'tbl_9': 7.372,
     'tbl_10': 6.948,
     'tbl_11': 6.943,
     'tbl_12': 7.082,
     'tbl_13': 6.895,
     'tbl_14': 7.407,
     'tbl_15': 6.983,
     'tbl_16': 7.253,
     'tbl_17': 5.909,
     'tbl_18': 7.231,
     'tbl_19': 7.103,
     'tbl_20': 7.824,
     'tbl_21': 7.508,
     'tbl_22': 6.78,
     'tbl_23': 6.276,
     'tbl_24': 7.021,
     'tbl_25': 6.583,
     'tbl_26': 6.925,
     'tbl_27': 6.875,
     'tbl_28': 7.012,
     'tbl_29': 7.216,
     'tbl_30': 6.962,
     'tbl_31': 6.848,
     'tbl_32': 7.447,
     'tbl_33': 6.423,
     'tbl_34': 7.396,
     'tbl_35': 6.298,
     'tbl_36': 6.838,
     'tbl_37': 6.239,
     'tbl_38': 7.211,
     'tbl_39': 6.475,
     'L0_rec_k1': 8.0,
     'L0_rec_k2': 8.0}
    for name, (base, spread) in spreads.items():
        noise = np.random.default_rng([zlib.crc32(name.encode()), seed]).standard_normal(out[name].shape)
        drawn = base * np.exp(spread * noise) if base else spread * noise
        out[name] = jnp.asarray(drawn.astype(out[name].dtype))
    for name, factor in factors.items():
        out[name] = (out[name] * factor).astype(out[name].dtype)
    return out
```

```python
from contextlib import ExitStack

import concourse.bass as bass
from concourse import mybir

B, M, D, H = 512, 40, 16, 128
P = 128
BT = B // P
DG = 4
GROUPS = D // DG
COLS = DG * P
SH = 3
ROWS = SH * M
NPAIR = (M // 2 + 1) // SH
EXT = ROWS + NPAIR - 1
MB = COLS // H
NB = M // MB
NE = NB // 2
KB = P // D
NK = D
GW = KB * M + KB
F1, F2 = 512, 256
ND = 16
O1, O2 = F1 // P, F2 // P
MACS = NE * MB

F32 = mybir.dt.float32
F32R = mybir.dt.float32r
I32 = mybir.dt.int32
ALU = mybir.AluOpType
ACT = mybir.ActivationFunctionType
AX = mybir.AxisListType


def build(nc, ids, tables, dense_t, k0a, k0b, k1, k2, w1, w1d, b1, w2, b2, w3, ident_in, mask_in, out):
    with ExitStack() as ctx:
        def sb(name, shape, dt=F32):
            return ctx.enter_context(nc.sbuf_tensor(name, shape, dt))

        def sem(name):
            return ctx.enter_context(nc.semaphore(name))

        pairs = sb("pairs", [ROWS, NPAIR * H])
        k1_hi = sb("k1_hi", [H, M * H], F32R)
        k1_lo = sb("k1_lo", [H, M * H], F32R)
        k2_sb = sb("k2_sb", [H, M * H])
        w1_sb = sb("w1_sb", [P, 3, F1])
        w1d_sb = sb("w1d_sb", [ND, F1])
        w2_sb = sb("w2_sb", [P, O1, F2])
        w3_sb = sb("w3_sb", [P, O2])
        b1_sb = sb("b1_sb", [P, O1])
        b2_sb = sb("b2_sb", [P, O2])
        ident = sb("ident", [P, P])
        mask = sb("mask", [P, KB])
        idx = sb("idx", [P, M], I32)
        emb_raw = sb("emb_raw", [P, M * D])
        emb = sb("emb", [P, EXT * D])
        emb_first = sb("emb_first", [P, ROWS * D])
        emb_sc = sb("emb_sc", [P, M * D])
        x0_rep = sb("x0_rep", [ROWS, COLS])
        x0_t = sb("x0_t", [M, P * D])
        prod = sb("prod", [ROWS, 2, COLS])
        x1_sb = sb("x1_sb", [H, COLS])
        x1_hi = sb("x1_hi", [H, COLS], F32R)
        x1_lo = sb("x1_lo", [H, COLS], F32R)
        z0_part = sb("z0_part", [H, GROUPS, P])
        z0_sb = sb("z0_sb", [H, P])
        scaled = sb("scaled", [P, 2, NE * COLS])
        sums = sb("sums", [P, 2, 2 * MB, H])
        x2_t = sb("x2_t", [P, D * H])
        x2_g = sb("x2_g", [P, NK * H])
        x0_g = sb("x0_g", [P, NK * M])
        blocks = sb("blocks", [P, NK, GW])
        gram = sb("gram", [H, NK, GW])
        dense_sb = sb("dense_sb", [ND, P])
        y_sb = sb("y_sb", [1, P])
        scratch = nc.dram_tensor("x2_scratch", [P, D * H], F32, kind="Internal").ap()
        h1_sb = x2_g[:, 0:F1].rearrange("p (o b) -> p o b", o=O1)
        h2_sb = x2_g[:, F1:F1 + F2].rearrange("p (o b) -> p o b", o=O2)
        z2_sb = x2_g[:, F1 + F2:F1 + F2 + P]
        pairs_b = prod[:].rearrange("p a c -> p (a c)")[:, 0:NPAIR * H]
        k1_stage = scaled[:].rearrange("p a c -> p (a c)")

        ps = [ctx.enter_context(nc.psum_tensor(n, [P, COLS], F32))
              for n in ("ps_yd0", "ps_yd1", "ps_ya0", "ps_ya1", "ps_s0", "ps_s1", "ps_x1", "ps_tail")]
        ps_yd, ps_ya, ps_s, ps_x1, ps_tail = ps[0:2], ps[2:4], ps[4:6], ps[6], ps[7]

        idx_in = sem("idx_in")
        small_in = sem("small_in")
        k1_in = sem("k1_in")
        late_in = sem("late_in")
        gathered = sem("gathered")
        pairs_ready = sem("pairs_ready")
        k1h_ready = sem("k1h_ready")
        k1l_ready = sem("k1l_ready")
        blocks_zeroed = sem("blocks_zeroed")
        blocks_init = sem("blocks_init")
        emb_ready = sem("emb_ready")
        scal_ready = sem("scal_ready")
        rep_full = sem("rep_full")
        rep_ready = sem("rep_ready")
        shift_full = sem("shift_full")
        prod_ready = sem("prod_ready")
        pair_mm = sem("pair_mm")
        x1_ready = sem("x1_ready")
        x1h_ready = sem("x1h_ready")
        x1l_ready = sem("x1l_ready")
        yd_full = sem("yd_full")
        ya_full = sem("ya_full")
        mac_done = sem("mac_done")
        scaled_ready = sem("scaled_ready")
        pool_added = sem("pool_added")
        x2_ready = sem("x2_ready")
        x2_stored = sem("x2_stored")
        x2g_in = sem("x2g_in")
        x0g_full = sem("x0g_full")
        x0g_ready = sem("x0g_ready")
        blocks_in = sem("blocks_in")
        gram_full = sem("gram_full")
        gram_ready = sem("gram_ready")
        z0_ready = sem("z0_ready")
        z0_parts = sem("z0_parts")
        z2_full = sem("z2_full")
        z2_ready = sem("z2_ready")
        dense_in = sem("dense_in")
        h1_full = sem("h1_full")
        h1_ready = sem("h1_ready")
        h2_full = sem("h2_full")
        h2_ready = sem("h2_ready")
        y_full = sem("y_full")
        y_ready = sem("y_ready")
        y_stored = sem("y_stored")

        emb_v = emb[:].rearrange("p (m d) -> p m d", d=D)
        first_v = emb_first[:].rearrange("p (m d) -> p m d", d=D)
        raw_v = emb_raw[:].rearrange("p (m d) -> p m d", d=D)
        sc_v = emb_sc[:].rearrange("p (m d) -> p m d", d=D)
        gram_v = gram[:, :, 0:KB * M].rearrange("h k (b m) -> h k b m", b=KB)
        x0t_v = x0_t[:].rearrange("m (b d) -> m d b", d=D)
        out_v = out.rearrange("(t b) o -> t (o b)", t=BT)

        def scalar_of(m, d):
            return emb_sc[:, m * D + d:m * D + d + 1]

        block = ctx.enter_context(nc.Block())

        @block.sync
        def _(sp):
            sp.dma_start(idx[:], ids[0:P, :]).then_inc(idx_in, 16)
            for dst, src in ((ident, ident_in), (pairs, k0a), (pairs_b, k0b), (mask, mask_in)):
                sp.dma_start(dst if dst is pairs_b else dst[:], src).then_inc(small_in, 16)
            sp.dma_start(k1_stage, k1).then_inc(k1_in, 16)
            for dst, src in ((k2_sb, k2), (w1_sb, w1), (w1d_sb, w1d), (w2_sb, w2), (w3_sb, w3),
                             (b1_sb, b1), (b2_sb, b2)):
                sp.dma_start(dst[:], src).then_inc(late_in, 16)

            def store_x2(bt, dq):
                g = bt * GROUPS + dq
                sp.wait_ge(x2_ready, (g + 1) * DG)
                sp.nop(nofuse=True)
                if dq == 0:
                    sp.wait_ge(x2g_in, bt * 16)
                    sp.nop(nofuse=True)
                sl = slice(dq * DG * H, (dq + 1) * DG * H)
                sp.dma_start(scratch[:, sl], x2_t[:, sl]).then_inc(x2_stored, 16)
                sp.wait_ge(x2_stored, (g + 1) * 16)
                sp.nop(nofuse=True)

            def load_x2_g(t):
                src = bass.AP(scratch.tensor, 0, [[H, P], [KB * D * H, NK], [1, H]])
                sp.dma_start(x2_g[:].rearrange("p (k o) -> p k o", k=NK), src).then_inc(x2g_in, 16)
                sp.dma_start(dense_sb[:], dense_t[:, bass.ds(t * P, P)]).then_inc(dense_in, 16)

            def lay_blocks(bt):
                sp.wait_ge(x0g_ready, 2 * (bt + 1))
                sp.nop(nofuse=True)
                sp.wait_ge(gram_full, bt * NK)
                sp.nop(nofuse=True)
                if isinstance(bt, int) and bt == 0:
                    sp.wait_ge(blocks_init, 1)
                xv = x0_g[:].rearrange("p (k m) -> p k m", k=NK)
                for i in range(KB):
                    rows = slice(i * D, (i + 1) * D)
                    sp.dma_start(blocks[rows, :, i * M:(i + 1) * M], xv[rows]).then_inc(blocks_in, 16)

            def store_y(t):
                sp.wait_ge(y_ready, t + 1)
                sp.nop(nofuse=True)
                sp.dma_start(out_v[bass.ds(t, 1), :], y_sb[:]).then_inc(y_stored, 16)
                sp.wait_ge(y_stored, 16 * (t + 1))
                sp.nop(nofuse=True)

            def iteration(bt, tail):
                if tail:
                    store_x2(bt - 1, GROUPS - 1)
                    load_x2_g(bt - 1)
                store_x2(bt, 0)
                store_x2(bt, 1)
                lay_blocks(bt)
                store_x2(bt, 2)
                if tail:
                    store_y(bt - 1)

            iteration(0, False)
            with sp.Fori(1, BT) as bt:
                iteration(bt, True)
            store_x2(BT - 1, GROUPS - 1)
            load_x2_g(BT - 1)
            store_y(BT - 1)

        @block.tensor
        def _(pe):
            def replicas(L, t):
                pe.wait_ge(emb_ready, t + 1)
                pe.wait_ge(prod_ready, L * NPAIR)

            def transposes(bank, fields, dq, signal):
                for i in range(DG):
                    ins = pe.transpose(bank[0:ROWS, i * P:(i + 1) * P], fields[:, :, dq * DG + i], ident[:])
                ins.then_inc(signal, 1)

            def shifted(L, t, dq):
                if t == 1:
                    pe.wait_ge(rep_ready, L + 1)
                elif t > 1:
                    pe.wait_ge(prod_ready, L * NPAIR + t - 1)
                transposes(ps_s[(t + 1) % 2], emb_v[:, t:t + ROWS, :], dq, shift_full)

            def pair_matmul(L, t):
                if t == 0:
                    pe.wait_ge(x1_ready, L)
                pe.wait_ge(prod_ready, L * NPAIR + t + 1)
                pe.matmul(ps_x1[:], pairs[:, t * H:(t + 1) * H], prod[:, t % 2, :],
                          start=(t == 0), stop=(t == NPAIR - 1)).then_inc(pair_mm, 1)

            def bank(g, j, n):
                q = NB * j + n
                e = q // 2
                side, full, read = ((ps_yd, yd_full, mac_done), (ps_ya, ya_full, scaled_ready))[q % 2]
                if n == 0:
                    pe.wait_ge(x1l_ready, g * DG + j + 1)
                if not (isinstance(g, int) and g == 0 and e < 2):
                    done = g * (DG * NE) + e - 1
                    pe.wait_ge(read, done * MB if q % 2 == 0 else done)
                y = side[e % 2]
                hi, lo = x1_hi[:, j * P:(j + 1) * P], x1_lo[:, j * P:(j + 1) * P]
                ks = slice(n * COLS, (n + 1) * COLS)
                pe.matmul(y[:], hi, k1_hi[:, ks], start=True, stop=False)
                pe.matmul(y[:], hi, k1_lo[:, ks], start=False, stop=False)
                ins = pe.matmul(y[:], lo, k1_hi[:, ks], start=False, stop=True)
                ins.then_inc(full, 1)

            def gram_block(t, k):
                if k == 0:
                    pe.wait_ge(x0g_ready, 2 * (t + 1))
                    pe.wait_ge(x2g_in, 16 * (t + 1))
                    pe.wait_ge(blocks_in, 16 * KB * (t + 1))
                else:
                    pe.wait_ge(gram_ready, t * NK + k)
                pe.matmul(ps_tail[:, 0:GW], x2_g[:, k * H:(k + 1) * H], blocks[:, k, :],
                          start=True, stop=True).then_inc(gram_full, 1)

            def x0_blocks(bt, half):
                if half == 0:
                    pe.wait_ge(rep_ready, (bt + 1) * GROUPS)
                    pe.nop(nofuse=True)
                    pe.wait_ge(gram_ready, bt * NK)
                    pe.nop(nofuse=True)
                else:
                    pe.wait_ge(x0g_ready, 2 * bt + 1)
                    pe.nop(nofuse=True)
                for i in range(NK // 2):
                    k = half * (NK // 2) + i
                    ins = pe.transpose(ps_tail[:, i * M:(i + 1) * M], x0_t[:, k * P:(k + 1) * P],
                                       ident[0:M, 0:M])
                ins.then_inc(x0g_full, 1)

            def layer2(t, m0, m1, last=False):
                if m0 == 0:
                    pe.wait_ge(gram_ready, (t + 1) * NK)
                    if not last:
                        pe.wait_ge(x0g_ready, 2 * (t + 2))
                for m in range(m0, m1):
                    ins = pe.matmul(ps_tail[:, 0:P].rearrange("o (k b) -> o k b", k=NK), k2_sb[:, m * H:(m + 1) * H],
                                    gram_v[:, :, :, m], start=(m == 0), stop=(m == M - 1))
                if m1 == M:
                    ins.then_inc(z2_full, 1)

            def mlp1(t, o):
                if o == 0:
                    pe.wait_ge(z2_ready, t + 1)
                    pe.wait_ge(z0_ready, t + 1)
                    pe.wait_ge(dense_in, 16 * (t + 1))
                dst = ps_tail[:, o * P:(o + 1) * P]
                fs = slice(o * P, (o + 1) * P)
                pe.matmul(dst, w1_sb[:, 0, fs], z0_sb[:], start=True, stop=False)
                pe.matmul(dst.rearrange("o (k b) -> o k b", k=NK), w1_sb[:, 1, fs], gram[:, :, KB * M:GW],
                          start=False, stop=False)
                pe.matmul(dst, w1d_sb[:, fs], dense_sb[:], start=False, stop=False)
                ins = pe.matmul(dst, w1_sb[:, 2, fs], z2_sb, start=False, stop=True)
                if o == O1 - 1:
                    ins.then_inc(h1_full, 1)

            def mlp2(t, o):
                if o == 0:
                    pe.wait_ge(h1_ready, t + 1)
                for i in range(O1):
                    ins = pe.matmul(ps_tail[:, o * P:(o + 1) * P], w2_sb[:, i, o * P:(o + 1) * P],
                                    h1_sb[:, i, :], start=(i == 0), stop=(i == O1 - 1))
                if o == O2 - 1:
                    ins.then_inc(h2_full, 1)

            def mlp3(t):
                pe.wait_ge(h2_ready, t + 1)
                for i in range(O2):
                    ins = pe.matmul(ps_tail[0:1, 0:P], w3_sb[:, i:i + 1], h2_sb[:, i, :],
                                    start=(i == 0), stop=(i == O2 - 1))
                ins.then_inc(y_full, 1)

            def iteration(bt, tail, more):
                for dq in range(GROUPS):
                    g = bt * GROUPS + dq
                    L, dq1 = g + 1, (dq + 1) % GROUPS
                    t1 = bt + 1 if dq == GROUPS - 1 else bt
                    ahead = more or dq < GROUPS - 1
                    for j in range(DG):
                        for n in range(NB):
                            q = NB * j + n
                            bank(g, j, n)
                            if ahead:
                                if q == 0:
                                    replicas(L, t1)
                                    transposes(ps_s[0], first_v, dq1, rep_full)
                                if q % 4 == 2 and q < 4 * NPAIR:
                                    shifted(L, q // 4, dq1)
                                if q % 4 == 2 and 1 <= q // 4 <= NPAIR:
                                    pair_matmul(L, q // 4 - 1)
                            if tail and dq == 1 and q % 2 == 1 and 3 <= q < 3 + 2 * NK:
                                gram_block(bt - 1, (q - 3) // 2)
                            if dq == 2 and q in (4, 8):
                                x0_blocks(bt, q // 4 - 1)
                            if tail and dq == 2 and 12 <= q < 32:
                                layer2(bt - 1, (q - 12) * M // 20, (q - 11) * M // 20)
                            if tail and dq == 3 and q in (5, 7, 9, 11):
                                mlp1(bt - 1, (q - 5) // 2)
                            if tail and dq == 3 and q in (17, 19):
                                mlp2(bt - 1, (q - 17) // 2)
                            if tail and dq == 3 and q == 25:
                                mlp3(bt - 1)

            pe.wait_ge(small_in, 64)
            replicas(0, 0)
            transposes(ps_s[0], first_v, 0, rep_full)
            pe.wait_ge(pairs_ready, 1)
            shifted(0, 0, 0)
            for t in range(NPAIR):
                if t + 1 < NPAIR:
                    shifted(0, t + 1, 0)
                pair_matmul(0, t)
            pe.wait_ge(k1l_ready, 1)
            iteration(0, False, True)
            pe.wait_ge(late_in, 16 * 7)
            with pe.Fori(1, BT - 1) as bt:
                iteration(bt, True, True)
            iteration(BT - 1, True, False)
            t = BT - 1
            for k in range(NK):
                gram_block(t, k)
            layer2(t, 0, M, last=True)
            for o in range(O1):
                mlp1(t, o)
            for o in range(O2):
                mlp2(t, o)
            mlp3(t)

        @block.vector
        def _(dve):
            def macs(g, dq, j, e):
                dve.wait_ge(yd_full, g * (DG * NE) + j * NE + e + 1)
                y = ps_yd[(j * NE + e) % 2]
                for i in range(MB):
                    m = 2 * e * MB + i
                    acc = sums[:, j % 2, i, :]
                    yi = y[:, i * H:(i + 1) * H]
                    s = scalar_of(m, dq * DG + j)
                    if e == 0:
                        ins = dve.tensor_scalar(acc, yi, s, None, ALU.mult)
                    else:
                        dve.wait_ge(mac_done, g * (DG * MACS) + j * MACS + (e - 1) * MB + i + 1)
                        ins = dve.scalar_tensor_tensor(out=acc, in0=yi, scalar=s, in1=acc, op0=ALU.mult, op1=ALU.add)
                    ins.then_inc(mac_done, 1)

            def reduce_x2(g, dq, j):
                tile = g * DG + j
                dve.wait_ge(mac_done, (tile + 1) * MACS)
                dve.wait_ge(pool_added, (tile + 1) * (NE - 1))
                if dq == GROUPS - 1:
                    dve.wait_ge(x2_stored, g * 16)
                elif not (isinstance(g, int) and g < GROUPS):
                    dve.wait_ge(x2_stored, (g - GROUPS + 1) * 16)
                d = dq * DG + j
                dve.tensor_reduce(x2_t[:, d * H:(d + 1) * H], sums[:, j % 2].rearrange("p s o -> p o s"),
                                  AX.X, ALU.add).then_inc(x2_ready, 1)

            def product(L, t):
                dve.wait_ge(shift_full, L * NPAIR + t + 1)
                if t == 0:
                    dve.wait_ge(rep_ready, L + 1)
                if t < 2:
                    dve.wait_ge(pair_mm, L * NPAIR)
                else:
                    dve.wait_ge(pair_mm, L * NPAIR + t - 1)
                dve.tensor_tensor(prod[:, t % 2, :], ps_s[(t + 1) % 2][0:ROWS, :], x0_rep[:],
                                  ALU.mult).then_inc(prod_ready, 1)

            def x1_low(L, j0, j1):
                dve.wait_ge(x1h_ready, L * DG + j1)
                cs = slice(j0 * P, j1 * P)
                dve.tensor_tensor(x1_lo[:, cs], x1_sb[:, cs], x1_hi[:, cs].bitcast(F32),
                                  ALU.subtract).then_inc(x1l_ready, j1 - j0)

            def z0_sum(L, dq):
                dve.wait_ge(x1_ready, L + 1)
                dve.tensor_reduce(z0_part[:, dq, :], x1_sb[:].rearrange("h (d b) -> h b d", d=DG),
                                  AX.X, ALU.add).then_inc(z0_parts, 1)

            def z0_total(t):
                dve.wait_ge(h1_full, t)
                dve.wait_ge(z0_parts, (t + 1) * GROUPS)
                dve.tensor_reduce(z0_sb[:], z0_part[:].rearrange("h q b -> h b q"), AX.X,
                                  ALU.add).then_inc(z0_ready, 1)

            def iteration(bt, more):
                for dq in range(GROUPS):
                    g = bt * GROUPS + dq
                    L, dq1 = g + 1, (dq + 1) % GROUPS
                    ahead = more or dq < GROUPS - 1
                    dve.wait_ge(scal_ready, g + 1)
                    for j in range(DG):
                        for e in range(NE):
                            a = j * NE + e
                            macs(g, dq, j, e)
                            if a == 1:
                                x1_low(g, DG - 1, DG)
                            if ahead and a % 2 == 1 and a < 2 * NPAIR:
                                product(L, a // 2)
                            if e == 2 and j > 0:
                                reduce_x2(g, dq, j - 1)
                            if e == 2 and j == 0 and not (isinstance(g, int) and g == 0):
                                reduce_x2(g - 1, (dq - 1) % GROUPS, DG - 1)
                            if a == 16 and dq == GROUPS - 1:
                                z0_total(bt)
                            if a == 17 and ahead:
                                if dq1 == 0:
                                    dve.wait_ge(z0_ready, bt + 1)
                                z0_sum(L, dq1)
                                x1_low(L, 0, DG - 1)

            dve.memset(blocks[:], 0.0).then_inc(blocks_zeroed, 1)
            dve.wait_ge(small_in, 64)
            dve.tensor_tensor(pairs[:], pairs[:], pairs_b, ALU.add).then_inc(pairs_ready, 1)
            dve.wait_ge(blocks_zeroed, 1)
            dve.tensor_copy(blocks[:, :, KB * M:GW], mask[:].unsqueeze(1).to_broadcast([P, NK, KB])).then_inc(blocks_init, 1)
            dve.wait_ge(k1h_ready, 1)
            dve.tensor_tensor(k1_lo[:], k1_stage, k1_hi[:].bitcast(F32), ALU.subtract).then_inc(k1l_ready, 1)
            for t in range(NPAIR):
                product(0, t)
            z0_sum(0, 0)
            x1_low(0, 0, DG - 1)
            iteration(0, True)
            with dve.Fori(1, BT - 1) as bt:
                iteration(bt, True)
            iteration(BT - 1, False)
            reduce_x2(BT * GROUPS - 1, GROUPS - 1, DG - 1)

        @block.scalar
        def _(act):
            def scale_bank(g, dq, j, a):
                e = a - j * NE
                tile = g * DG + j
                act.wait_ge(ya_full, g * (DG * NE) + a + 1)
                if not (isinstance(g, int) and g * DG + j < 2):
                    act.wait_ge(pool_added, (tile - 1) * (NE - 1))
                y = ps_ya[a % 2]
                for i in range(MB):
                    m = (2 * e + 1) * MB + i
                    at = e * COLS + i * H
                    ins = act.activation(scaled[:, j % 2, at:at + H], y[:, i * H:(i + 1) * H], ACT.Copy,
                                         scale=scalar_of(m, dq * DG + j))
                ins.then_inc(scaled_ready, 1)

            def replicas_out(L, dq):
                act.wait_ge(rep_full, L + 1)
                act.wait_ge(prod_ready, L * NPAIR)
                act.activation(x0_rep[:], ps_s[0][0:ROWS, :], ACT.Copy)
                if dq == 0:
                    act.wait_ge(x0g_full, 2 * batch_of(L))
                act.activation(x0t_v[:, dq * DG:(dq + 1) * DG, :],
                               ps_s[0][0:M, :].rearrange("m (d b) -> m d b", d=DG), ACT.Copy).then_inc(rep_ready, 1)

            def batch_of(L):
                return L // GROUPS if isinstance(L, int) else cur[0] + 1

            cur = [0]

            def x1_out(L):
                act.wait_ge(pair_mm, (L + 1) * NPAIR)
                act.wait_ge(z0_parts, L)
                act.wait_ge(x1l_ready, L * DG)
                act.activation(x1_sb[:], ps_x1[:], ACT.Copy).then_inc(x1_ready, 1)

            def x1_high(L, j0, j1):
                act.wait_ge(x1_ready, L + 1)
                if not (isinstance(L, int) and L == 0):
                    act.wait_ge(ya_full, (L - 1) * (DG * NE) + j1 * NE)
                cs = slice(j0 * P, j1 * P)
                act.activation(x1_hi[:, cs], x1_sb[:, cs], ACT.Copy).then_inc(x1h_ready, j1 - j0)

            def take_embeddings(t):
                act.wait_ge(gathered, (t + 1) * M * 16)
                act.wait_ge(shift_full, t * GROUPS * NPAIR)
                act.wait_ge(scal_ready, t * GROUPS)
                for j in range(SH):
                    first = (-NPAIR * j) % M * D
                    at = j * M * D
                    if first:
                        act.activation(emb_first[:, at:at + M * D - first], emb_raw[:, first:], ACT.Copy)
                    act.activation(emb_first[:, at + (M * D - first) % (M * D):at + M * D], emb_raw[:, 0:first or M * D], ACT.Copy)
                for at in range(0, EXT * D, M * D):
                    n = min(M * D, EXT * D - at)
                    ins = act.activation(emb[:, at:at + n], emb_raw[:, 0:n], ACT.Copy)
                ins.then_inc(emb_ready, 1)

            def take_scalars(t, dq):
                act.wait_ge(emb_ready, t + 1)
                if not (isinstance(t, int) and t == 0):
                    act.wait_ge(mac_done, ((t - 1) * GROUPS + dq + 1) * DG * MACS)
                ds = slice(dq * DG, (dq + 1) * DG)
                act.activation(sc_v[:, :, ds], emb_v[:, 0:M, ds], ACT.Copy).then_inc(scal_ready, 1)

            def x0g_out(bt, half):
                act.wait_ge(x0g_full, 2 * bt + half + 1)
                act.wait_ge(blocks_in, 16 * KB * bt)
                w = NK // 2 * M
                act.activation(x0_g[:, half * w:(half + 1) * w], ps_tail[:, 0:w], ACT.Copy).then_inc(x0g_ready, 1)

            def gram_out(t, k):
                act.wait_ge(gram_full, t * NK + k + 1)
                act.activation(gram[:, k, :], ps_tail[:, 0:GW], ACT.Copy).then_inc(gram_ready, 1)

            def z2_out(t):
                act.wait_ge(z2_full, t + 1)
                act.activation(z2_sb, ps_tail[:, 0:P], ACT.Copy).then_inc(z2_ready, 1)

            def relu(t, full, ready, dst, bias, n):
                act.wait_ge(full, t + 1)
                for o in range(n):
                    ins = act.activation(dst[:, o, :], ps_tail[:, o * P:(o + 1) * P], ACT.Relu, bias=bias[:, o:o + 1])
                ins.then_inc(ready, 1)

            def y_out(t):
                act.wait_ge(y_full, t + 1)
                act.activation(y_sb[:], ps_tail[0:1, 0:P], ACT.Copy).then_inc(y_ready, 1)

            def iteration(bt, tail, more):
                cur[0] = bt
                for dq in range(GROUPS):
                    g = bt * GROUPS + dq
                    L, dq1 = g + 1, (dq + 1) % GROUPS
                    ahead = more or dq < GROUPS - 1
                    if dq == 0 and more:
                        act.dma_start(idx[:], ids[bass.ds((bt + 1) * P, P), :]).then_inc(idx_in, 16)
                    if dq == 3 and more:
                        take_embeddings(bt + 1)
                    for j in range(DG):
                        for e in range(NE):
                            a = j * NE + e
                            if a == 0:
                                act.wait_ge(scal_ready, g + 1)
                            scale_bank(g, dq, j, a)
                            if a == 0 and ahead:
                                replicas_out(L, dq1)
                            if a == 1:
                                x1_high(g, DG - 1, DG)
                            if a == 6 and dq == 3 and more:
                                for s in range(3):
                                    take_scalars(bt + 1, s)
                            if a == 6 and dq == 0:
                                if tail:
                                    take_scalars(bt, 3)
                            if tail and dq == 1 and 1 <= a < 1 + NK:
                                gram_out(bt - 1, a - 1)
                            if dq == 2 and a in (2, 4):
                                x0g_out(bt, a // 2 - 1)
                            if tail and dq == 2 and a == 16:
                                z2_out(bt - 1)
                            if tail and dq == 3 and a == 6:
                                relu(bt - 1, h1_full, h1_ready, h1_sb, b1_sb, O1)
                            if tail and dq == 3 and a == 10:
                                relu(bt - 1, h2_full, h2_ready, h2_sb, b2_sb, O2)
                            if tail and dq == 3 and a == 13:
                                y_out(bt - 1)
                            if a == 17 and ahead:
                                x1_out(L)
                                x1_high(L, 0, DG - 1)

            act.wait_ge(k1_in, 16)
            act.activation(k1_hi[:], k1_stage, ACT.Copy).then_inc(k1h_ready, 1)
            take_embeddings(0)
            for s in range(GROUPS):
                take_scalars(0, s)
            replicas_out(0, 0)
            x1_out(0)
            x1_high(0, 0, DG - 1)
            act.wait_ge(k1l_ready, 1)
            act.wait_ge(late_in, 16 * 7)
            iteration(0, False, True)
            with act.Fori(1, BT - 1) as bt:
                iteration(bt, True, True)
            iteration(BT - 1, True, False)
            t = BT - 1
            for k in range(NK):
                gram_out(t, k)
            z2_out(t)
            relu(t, h1_full, h1_ready, h1_sb, b1_sb, O1)
            relu(t, h2_full, h2_ready, h2_sb, b2_sb, O2)
            y_out(t)

        @block.gpsimd
        def _(pool):
            def gather(t, f):
                if f == 0:
                    pool.wait_ge(idx_in, 16 * (t + 1))
                    pool.nop(nofuse=True)
                    pool.wait_ge(emb_ready, t)
                    pool.nop(nofuse=True)
                pool.indirect_dma_start(emb_raw[:, f * D:(f + 1) * D], None, tables[f],
                                        bass.IndirectOffsetOnAxis(ap=idx[:, f:f + 1], axis=0)).then_inc(gathered, 16)

            def iteration(bt, more):
                for dq in range(GROUPS):
                    g = bt * GROUPS + dq
                    for j in range(DG):
                        tile = g * DG + j
                        dst = sums[:, j % 2, MB:2 * MB, :].rearrange("p s o -> p (s o)")
                        for e in range(1, NE):
                            pool.wait_ge(scaled_ready, g * (DG * NE) + j * NE + e + 1)
                            src = scaled[:, j % 2, e * COLS:(e + 1) * COLS]
                            if e == 1:
                                if not (isinstance(g, int) and g * DG + j < 2):
                                    pool.wait_ge(x2_ready, tile - 1)
                                other = scaled[:, j % 2, 0:COLS]
                            else:
                                pool.wait_ge(pool_added, tile * (NE - 1) + e - 1)
                                other = dst
                            pool.tensor_tensor(dst, src, other, ALU.add).then_inc(pool_added, 1)
                            slot = j * (NE - 1) + e - 1
                            f = dq * 14 + slot - 2
                            if more and dq < 3 and 2 <= slot and f < min(M, 14 * (dq + 1)):
                                gather(bt + 1, f)

            for f in range(M):
                gather(0, f)
            iteration(0, True)
            with pool.Fori(1, BT - 1) as bt:
                iteration(bt, True)
            iteration(BT - 1, False)


def kernel(**inputs):
    import numpy as np
    from concourse import bacc
    from concourse.bass_utils import run_bass_kernel_spmd

    a = {k: np.asarray(v) for k, v in inputs.items()}
    k0 = a["L0_rec_k0"]
    i, j = np.tile(np.arange(M), SH), np.repeat(np.arange(SH), M)
    h = (i - NPAIR * j) % M
    lay_a, lay_b = [], []
    for t in range(NPAIR):
        shift, m = NPAIR * j + t, (i + t) % M
        lay_a.append(k0[:, h, m].T)
        twice = np.isin(shift, (0, M // 2))
        lay_b.append(np.where(twice[:, None], np.zeros((), k0.dtype), k0[:, m, h].T))
    arrays = {
        "ids": a["ids"],
        "dense_t": np.ascontiguousarray(a["dense_ctx"].T),
        "k0a": np.ascontiguousarray(np.concatenate(lay_a, axis=1)),
        "k0b": np.ascontiguousarray(np.concatenate(lay_b, axis=1)),
        "k1": np.ascontiguousarray(a["L0_rec_k1"].transpose(1, 2, 0)).reshape(H, M * H),
        "k2": np.ascontiguousarray(a["L0_rec_k2"].transpose(1, 2, 0)).reshape(H, M * H),
        "w1": np.ascontiguousarray(a["W_top1"][:3 * P].reshape(3, P, F1).transpose(1, 0, 2)),
        "w1d": np.ascontiguousarray(a["W_top1"][3 * P:]),
        "b1": np.ascontiguousarray(a["b_top1"].reshape(O1, P).T),
        "w2": np.ascontiguousarray(a["W_top2"].reshape(O1, P, F2).transpose(1, 0, 2)),
        "b2": np.ascontiguousarray(a["b_top2"].reshape(O2, P).T),
        "w3": np.ascontiguousarray(a["W_top3"].reshape(O2, P).T),
        "ident_in": np.eye(P, dtype=np.float32),
        "mask_in": np.kron(np.eye(KB, dtype=np.float32), np.ones((D, 1), np.float32)),
    }
    tables = {f"tbl_{f}": a[f"tbl_{f}"] for f in range(M)}
    nc = bacc.Bacc("TRN2", target_bir_lowering=False, num_devices=1)

    def dram(name, array):
        return nc.dram_tensor(name, array.shape, mybir.dt.from_np(array.dtype), kind="ExternalInput").ap()

    args = {name: dram(name, array) for name, array in arrays.items()}
    tabs = [dram(name, array) for name, array in tables.items()]
    out = nc.dram_tensor("out", [B, 1], F32, kind="ExternalOutput").ap()
    build(nc, tables=tabs, out=out, **args)
    r = run_bass_kernel_spmd(nc, [{**arrays, **tables}], core_ids=[0])
    return r.results[0]["out"]
```

```python
from contextlib import ExitStack

import concourse.bass as bass
from concourse import mybir

B, M, D, H = 512, 40, 16, 128
P = 128
BT = B // P
DG = 4
GROUPS = D // DG
COLS = DG * P
SH = 3
LOW = 64
ROWS = SH * M
NPAIR = (M // 2 + 1) // SH
MB = COLS // H
NB = M // MB
NE = NB // 2
KB = P // D
NK = D
GW = KB * M + KB
F1, F2 = 512, 256
ND = 16
O1, O2 = F1 // P, F2 // P
MACS = NE * MB

F32 = mybir.dt.float32
F32R = mybir.dt.float32r
I32 = mybir.dt.int32
ALU = mybir.AluOpType
ACT = mybir.ActivationFunctionType
AX = mybir.AxisListType


def build(nc, ids, tables, dense_t, k0a, k0b, k1, k2, w1, w1d, b1, w2, b2, w3, ident_in, mask_in, select_in, out):
    with ExitStack() as ctx:
        def sb(name, shape, dt=F32):
            return ctx.enter_context(nc.sbuf_tensor(name, shape, dt))

        def sem(name):
            return ctx.enter_context(nc.semaphore(name))

        pairs_hi = sb("pairs_hi", [ROWS, NPAIR * H], F32R)
        pairs_lo = sb("pairs_lo", [ROWS, NPAIR * H], F32R)
        select = sb("select", [LOW + M, (NPAIR + 1) * ROWS], F32R)
        k1_hi = sb("k1_hi", [H, M * H], F32R)
        k1_lo = sb("k1_lo", [H, M * H], F32R)
        k2_sb = sb("k2_sb", [H, M * H])
        w1_sb = sb("w1_sb", [P, 3, F1])
        w2_sb = sb("w2_sb", [P, O1, F2])
        w3_sb = sb("w3_sb", [P, O2])
        b1_sb = sb("b1_sb", [P, O1])
        b2_sb = sb("b2_sb", [P, O2])
        ident = sb("ident", [P, P])
        mask = sb("mask", [P, KB])
        idx = sb("idx", [P, M], I32)
        emb_raw = sb("emb_raw", [P, M * D])
        emb = sb("emb", [P, M * D])
        emb_sc = sb("emb_sc", [P, M * D])
        x0_rep = sb("x0_rep", [ROWS, COLS])
        x0_and_dense = sb("x0_and_dense", [LOW + ND, P * D])
        x0_t = x0_and_dense[0:M, :]
        x0_split = sb("x0_split", [LOW + M, COLS], F32R)
        prod = sb("prod", [ROWS, 2, COLS])
        prod_hi = sb("prod_hi", [ROWS, 2, COLS], F32R)
        prod_lo = sb("prod_lo", [ROWS, 2, COLS], F32R)
        x1_sb = sb("x1_sb", [H, COLS])
        x1_hi = sb("x1_hi", [H, COLS], F32R)
        x1_lo = sb("x1_lo", [H, COLS], F32R)
        z0_part = sb("z0_part", [H, GROUPS, P])
        z0_sb = sb("z0_sb", [H, P])
        scaled = sb("scaled", [P, 2, NE * COLS])
        sums = sb("sums", [P, 2, 2 * MB, H])
        x2_t = sb("x2_t", [P, D * H])
        x2_g = sb("x2_g", [P, NK * H])
        blocks = sb("blocks", [P, NK, GW])
        gram = sb("gram", [H, NK, GW])
        scratch = nc.dram_tensor("x2_scratch", [P, D * H], F32, kind="Internal").ap()
        h1_sb = x2_g[:, 0:F1].rearrange("p (o b) -> p o b", o=O1)
        h2_sb = x2_g[:, F1:F1 + F2].rearrange("p (o b) -> p o b", o=O2)
        z2_sb = x2_g[:, F1 + F2:F1 + F2 + P]
        y_sb = x2_g[0:1, F1 + F2 + P:F1 + F2 + 2 * P]
        x0_g = x2_g[:, F1 + F2 + 2 * P:F1 + F2 + 2 * P + NK * M]
        w1d_sb = x0_and_dense[LOW:LOW + ND, 0:F1]
        dense_sb = x0_and_dense[LOW:LOW + ND, F1:F1 + P]
        pairs_b = prod[:].rearrange("p a c -> p (a c)")[:, 0:NPAIR * H]
        select_stage = x2_t[0:LOW + M, 0:(NPAIR + 1) * ROWS]
        pairs = x2_t[0:ROWS, (NPAIR + 1) * ROWS:(NPAIR + 1) * ROWS + NPAIR * H]
        k1_stage = scaled[:].rearrange("p a c -> p (a c)")

        ps = [ctx.enter_context(nc.psum_tensor(n, [P, COLS], F32))
              for n in ("ps_yd0", "ps_yd1", "ps_ya0", "ps_ya1", "ps_s0", "ps_s1", "ps_x1", "ps_tail")]
        ps_yd, ps_ya, ps_s, ps_x1, ps_tail = ps[0:2], ps[2:4], ps[4:6], ps[6], ps[7]

        idx_in = sem("idx_in")
        small_in = sem("small_in")
        k1_in = sem("k1_in")
        late_in = sem("late_in")
        gathered = sem("gathered")
        pairs_ready = sem("pairs_ready")
        halves_ready = sem("halves_ready")
        split_zeroed = sem("split_zeroed")
        k1h_ready = sem("k1h_ready")
        k1l_ready = sem("k1l_ready")
        blocks_zeroed = sem("blocks_zeroed")
        blocks_init = sem("blocks_init")
        emb_ready = sem("emb_ready")
        scal_ready = sem("scal_ready")
        x0_full = sem("x0_full")
        x0h_ready = sem("x0h_ready")
        x0l_ready = sem("x0l_ready")
        rep_full = sem("rep_full")
        rep_ready = sem("rep_ready")
        shift_full = sem("shift_full")
        prod_ready = sem("prod_ready")
        prodh_ready = sem("prodh_ready")
        prodl_ready = sem("prodl_ready")
        pair_mm = sem("pair_mm")
        x1_ready = sem("x1_ready")
        x1h_ready = sem("x1h_ready")
        x1l_ready = sem("x1l_ready")
        yd_full = sem("yd_full")
        ya_full = sem("ya_full")
        mac_done = sem("mac_done")
        scaled_ready = sem("scaled_ready")
        pool_added = sem("pool_added")
        x2_ready = sem("x2_ready")
        x2_stored = sem("x2_stored")
        x2g_in = sem("x2g_in")
        x0g_full = sem("x0g_full")
        x0g_ready = sem("x0g_ready")
        blocks_in = sem("blocks_in")
        gram_full = sem("gram_full")
        gram_ready = sem("gram_ready")
        z0_ready = sem("z0_ready")
        z0_parts = sem("z0_parts")
        z2_full = sem("z2_full")
        z2_ready = sem("z2_ready")
        dense_in = sem("dense_in")
        h1_full = sem("h1_full")
        h1_ready = sem("h1_ready")
        h2_full = sem("h2_full")
        h2_ready = sem("h2_ready")
        y_full = sem("y_full")
        y_ready = sem("y_ready")
        y_stored = sem("y_stored")

        emb_v = emb[:].rearrange("p (m d) -> p m d", d=D)
        sc_v = emb_sc[:].rearrange("p (m d) -> p m d", d=D)
        gram_v = gram[:, :, 0:KB * M].rearrange("h k (b m) -> h k b m", b=KB)
        x0t_v = x0_t.rearrange("m (b d) -> m d b", d=D)
        out_v = out.rearrange("(t b) o -> t (o b)", t=BT)

        def scalar_of(m, d):
            return emb_sc[:, m * D + d:m * D + d + 1]

        last_banks = (ps_tail, ps_x1, *ps_s)

        block = ctx.enter_context(nc.Block())

        @block.sync
        def _(sp):
            sp.dma_start(idx[:], ids[0:P, :]).then_inc(idx_in, 16)
            for dst, src in ((ident, ident_in), (mask, mask_in)):
                sp.dma_start(dst[:], src).then_inc(small_in, 16)
            for dst, src in ((pairs, k0a), (pairs_b, k0b), (select_stage, select_in)):
                sp.dma_start(dst, src).then_inc(small_in, 16)
            sp.dma_start(k1_stage, k1).then_inc(k1_in, 16)
            for dst, src in ((k2_sb, k2), (w1_sb, w1), (w2_sb, w2), (w3_sb, w3),
                             (b1_sb, b1), (b2_sb, b2)):
                sp.dma_start(dst[:], src).then_inc(late_in, 16)
            sp.dma_start(w1d_sb, w1d).then_inc(late_in, 16)

            def store_x2(bt, dq):
                g = bt * GROUPS + dq
                sp.wait_ge(x2_ready, (g + 1) * DG)
                sp.nop(nofuse=True)
                if dq == 0:
                    sp.wait_ge(x2g_in, bt * 16)
                    sp.nop(nofuse=True)
                sl = slice(dq * DG * H, (dq + 1) * DG * H)
                sp.dma_start(scratch[:, sl], x2_t[:, sl]).then_inc(x2_stored, 16)
                sp.wait_ge(x2_stored, (g + 1) * 16)
                sp.nop(nofuse=True)

            def load_x2_g(t):
                sp.wait_ge(blocks_in, 16 * KB * (t + 1))
                sp.nop(nofuse=True)
                src = bass.AP(scratch.tensor, 0, [[H, P], [KB * D * H, NK], [1, H]])
                sp.dma_start(x2_g[:].rearrange("p (k o) -> p k o", k=NK), src).then_inc(x2g_in, 16)
                sp.dma_start(dense_sb, dense_t[:, bass.ds(t * P, P)]).then_inc(dense_in, 16)

            def lay_blocks(bt):
                sp.wait_ge(x0g_ready, 2 * (bt + 1))
                sp.nop(nofuse=True)
                sp.wait_ge(gram_full, bt * NK)
                sp.nop(nofuse=True)
                if isinstance(bt, int) and bt == 0:
                    sp.wait_ge(blocks_init, 1)
                xv = x0_g.rearrange("p (k m) -> p k m", k=NK)
                for i in range(KB):
                    rows = slice(i * D, (i + 1) * D)
                    sp.dma_start(blocks[rows, :, i * M:(i + 1) * M], xv[rows]).then_inc(blocks_in, 16)

            def store_y(t):
                sp.wait_ge(y_ready, t + 1)
                sp.nop(nofuse=True)
                sp.dma_start(out_v[bass.ds(t, 1), :], y_sb).then_inc(y_stored, 16)
                sp.wait_ge(y_stored, 16 * (t + 1))
                sp.nop(nofuse=True)

            def iteration(bt, tail):
                if tail:
                    store_x2(bt - 1, GROUPS - 1)
                    load_x2_g(bt - 1)
                store_x2(bt, 0)
                store_x2(bt, 1)
                lay_blocks(bt)
                store_x2(bt, 2)
                if tail:
                    store_y(bt - 1)

            iteration(0, False)
            with sp.Fori(1, BT) as bt:
                iteration(bt, True)
            store_x2(BT - 1, GROUPS - 1)
            load_x2_g(BT - 1)
            store_y(BT - 1)

        @block.tensor
        def _(pe):
            def x0_columns(L, t, dq):
                if dq == 0:
                    pe.wait_ge(emb_ready, t + 1)
                pe.wait_ge(prod_ready, L * NPAIR)
                pe.nop(nofuse=True)
                for i in range(DG):
                    ins = pe.transpose(ps_s[0][0:M, i * P:(i + 1) * P], emb_v[:, :, dq * DG + i], ident[:])
                ins.then_inc(x0_full, 1)

            def first_fields(L):
                pe.wait_ge(x0l_ready, L + 1)
                pe.matmul(ps_s[0][0:ROWS, :], select[:, 0:ROWS], x0_split[:],
                          start=True, stop=True).then_inc(rep_full, 1)

            def second_fields(L, t):
                if t == 1:
                    pe.wait_ge(rep_ready, L + 1)
                elif t > 1:
                    pe.wait_ge(prod_ready, L * NPAIR + t - 1)
                pe.matmul(ps_s[(t + 1) % 2][0:ROWS, :], select[:, (t + 1) * ROWS:(t + 2) * ROWS], x0_split[:],
                          start=True, stop=True).then_inc(shift_full, 1)

            def pair_matmul(L, t):
                if t == 0:
                    pe.wait_ge(x1_ready, L)
                pe.wait_ge(prodl_ready, L * NPAIR + t + 1)
                ks = slice(t * H, (t + 1) * H)
                pe.matmul(ps_x1[:], pairs_hi[:, ks], prod_hi[:, t % 2, :], start=(t == 0), stop=False)
                pe.matmul(ps_x1[:], pairs_lo[:, ks], prod_hi[:, t % 2, :], start=False, stop=False)
                pe.matmul(ps_x1[:], pairs_hi[:, ks], prod_lo[:, t % 2, :],
                          start=False, stop=(t == NPAIR - 1)).then_inc(pair_mm, 1)

            def bank(g, j, n):
                q = NB * j + n
                e = q // 2
                side, full, read = ((ps_yd, yd_full, mac_done), (ps_ya, ya_full, scaled_ready))[q % 2]
                if n == 0:
                    pe.wait_ge(x1l_ready, g * DG + j + 1)
                if not (isinstance(g, int) and g == 0 and e < 2):
                    done = g * (DG * NE) + e - 1
                    pe.wait_ge(read, done * MB if q % 2 == 0 else done)
                y = side[e % 2]
                hi, lo = x1_hi[:, j * P:(j + 1) * P], x1_lo[:, j * P:(j + 1) * P]
                ks = slice(n * COLS, (n + 1) * COLS)
                pe.matmul(y[:], hi, k1_hi[:, ks], start=True, stop=False)
                pe.matmul(y[:], hi, k1_lo[:, ks], start=False, stop=False)
                ins = pe.matmul(y[:], lo, k1_hi[:, ks], start=False, stop=True)
                ins.then_inc(full, 1)

            def gram_block(t, k, banks=(ps_tail,)):
                if k == 0:
                    pe.wait_ge(x0g_ready, 2 * (t + 1))
                    pe.wait_ge(x2g_in, 16 * (t + 1))
                    pe.wait_ge(blocks_in, 16 * KB * (t + 1))
                elif k >= len(banks):
                    pe.wait_ge(gram_ready, t * NK + k - len(banks) + 1)
                pe.matmul(banks[k % len(banks)][:, 0:GW], x2_g[:, k * H:(k + 1) * H], blocks[:, k, :],
                          start=True, stop=True).then_inc(gram_full, 1)

            def x0_blocks(bt, half):
                if half == 0:
                    pe.wait_ge(x0h_ready, (bt + 1) * GROUPS)
                    pe.nop(nofuse=True)
                    pe.wait_ge(gram_ready, bt * NK)
                    pe.nop(nofuse=True)
                else:
                    pe.wait_ge(x0g_ready, 2 * bt + 1)
                    pe.nop(nofuse=True)
                for i in range(NK // 2):
                    k = half * (NK // 2) + i
                    ins = pe.transpose(ps_tail[:, i * M:(i + 1) * M], x0_t[:, k * P:(k + 1) * P],
                                       ident[0:M, 0:M])
                ins.then_inc(x0g_full, 1)

            def layer2(t, m0, m1, last=False):
                if m0 == 0:
                    pe.wait_ge(gram_ready, (t + 1) * NK)
                    if not last:
                        pe.wait_ge(x0g_ready, 2 * (t + 2))
                for m in range(m0, m1):
                    ins = pe.matmul(ps_tail[:, 0:P].rearrange("o (k b) -> o k b", k=NK), k2_sb[:, m * H:(m + 1) * H],
                                    gram_v[:, :, :, m], start=(m == 0), stop=(m == M - 1))
                if m1 == M:
                    ins.then_inc(z2_full, 1)

            def mlp1(t, o):
                if o == 0:
                    pe.wait_ge(z2_ready, t + 1)
                    pe.wait_ge(z0_ready, t + 1)
                    pe.wait_ge(dense_in, 16 * (t + 1))
                dst = ps_tail[:, o * P:(o + 1) * P]
                fs = slice(o * P, (o + 1) * P)
                pe.matmul(dst, w1_sb[:, 0, fs], z0_sb[:], start=True, stop=False)
                pe.matmul(dst.rearrange("o (k b) -> o k b", k=NK), w1_sb[:, 1, fs], gram[:, :, KB * M:GW],
                          start=False, stop=False)
                pe.matmul(dst, w1d_sb[:, fs], dense_sb, start=False, stop=False)
                ins = pe.matmul(dst, w1_sb[:, 2, fs], z2_sb, start=False, stop=True)
                if o == O1 - 1:
                    ins.then_inc(h1_full, 1)

            def mlp2(t, o):
                if o == 0:
                    pe.wait_ge(h1_ready, t + 1)
                for i in range(O1):
                    ins = pe.matmul(ps_tail[:, o * P:(o + 1) * P], w2_sb[:, i, o * P:(o + 1) * P],
                                    h1_sb[:, i, :], start=(i == 0), stop=(i == O1 - 1))
                if o == O2 - 1:
                    ins.then_inc(h2_full, 1)

            def mlp3(t):
                pe.wait_ge(h2_ready, t + 1)
                for i in range(O2):
                    ins = pe.matmul(ps_tail[0:1, 0:P], w3_sb[:, i:i + 1], h2_sb[:, i, :],
                                    start=(i == 0), stop=(i == O2 - 1))
                ins.then_inc(y_full, 1)

            def iteration(bt, tail, more):
                for dq in range(GROUPS):
                    g = bt * GROUPS + dq
                    L = g + 1
                    ahead = more or dq < GROUPS - 1
                    for j in range(DG):
                        for n in range(NB):
                            q = NB * j + n
                            bank(g, j, n)
                            if ahead and q == 0:
                                first_fields(L)
                            if ahead and q % 4 == 1 and q < 4 * NPAIR:
                                second_fields(L, q // 4)
                            if ahead and q % 4 == 3 and 1 <= q // 4 <= NPAIR:
                                pair_matmul(L, q // 4 - 1)
                            if q == 33 and (more or dq < GROUPS - 2):
                                x0_columns(L + 1, bt + (dq + 2) // GROUPS, (dq + 2) % GROUPS)
                            if tail and dq == 1 and q % 2 == 1 and 3 <= q < 3 + 2 * NK:
                                gram_block(bt - 1, (q - 3) // 2)
                            if dq == 2 and q in (4, 8):
                                x0_blocks(bt, q // 4 - 1)
                            if tail and dq == 2 and 12 <= q < 32:
                                layer2(bt - 1, (q - 12) * M // 20, (q - 11) * M // 20)
                            if tail and dq == 3 and q in (5, 7, 9, 11):
                                mlp1(bt - 1, (q - 5) // 2)
                            if tail and dq == 3 and q in (17, 19):
                                mlp2(bt - 1, (q - 17) // 2)
                            if tail and dq == 3 and q == 25:
                                mlp3(bt - 1)

            pe.wait_ge(small_in, 16 * 5)
            x0_columns(0, 0, 0)
            pe.wait_ge(halves_ready, 3)
            first_fields(0)
            second_fields(0, 0)
            second_fields(0, 1)
            for t in range(NPAIR):
                if t + 2 < NPAIR:
                    second_fields(0, t + 2)
                pair_matmul(0, t)
            x0_columns(1, 0, 1)
            pe.wait_ge(k1l_ready, 1)
            iteration(0, False, True)
            pe.wait_ge(late_in, 16 * 7)
            with pe.Fori(1, BT - 1) as bt:
                iteration(bt, True, True)
            iteration(BT - 1, True, False)
            t = BT - 1
            for k in range(NK):
                gram_block(t, k, last_banks)
            layer2(t, 0, M, last=True)
            for o in range(O1):
                mlp1(t, o)
            for o in range(O2):
                mlp2(t, o)
            mlp3(t)

        @block.vector
        def _(dve):
            def macs(g, dq, j, e):
                dve.wait_ge(yd_full, g * (DG * NE) + j * NE + e + 1)
                y = ps_yd[(j * NE + e) % 2]
                for i in range(MB):
                    m = 2 * e * MB + i
                    acc = sums[:, j % 2, i, :]
                    yi = y[:, i * H:(i + 1) * H]
                    s = scalar_of(m, dq * DG + j)
                    if e == 0:
                        ins = dve.tensor_scalar(acc, yi, s, None, ALU.mult)
                    else:
                        dve.wait_ge(mac_done, g * (DG * MACS) + j * MACS + (e - 1) * MB + i + 1)
                        ins = dve.scalar_tensor_tensor(out=acc, in0=yi, scalar=s, in1=acc, op0=ALU.mult, op1=ALU.add)
                    ins.then_inc(mac_done, 1)

            def reduce_x2(g, dq, j):
                tile = g * DG + j
                dve.wait_ge(mac_done, (tile + 1) * MACS)
                dve.wait_ge(pool_added, (tile + 1) * (NE - 1))
                if dq == GROUPS - 1:
                    dve.wait_ge(x2_stored, g * 16)
                elif not (isinstance(g, int) and g < GROUPS):
                    dve.wait_ge(x2_stored, (g - GROUPS + 1) * 16)
                d = dq * DG + j
                dve.tensor_reduce(x2_t[:, d * H:(d + 1) * H], sums[:, j % 2].rearrange("p s o -> p o s"),
                                  AX.X, ALU.add).then_inc(x2_ready, 1)

            def product(L, t):
                dve.wait_ge(shift_full, L * NPAIR + t + 1)
                if t == 0:
                    dve.wait_ge(rep_ready, L + 1)
                if t < 2:
                    dve.wait_ge(prodl_ready, L * NPAIR)
                else:
                    dve.wait_ge(prodl_ready, L * NPAIR + t - 1)
                dve.tensor_tensor(prod[:, t % 2, :], ps_s[(t + 1) % 2][0:ROWS, :], x0_rep[:],
                                  ALU.mult).then_inc(prod_ready, 1)

            def product_low(L, t):
                n = L * NPAIR + t
                dve.wait_ge(prodh_ready, n + 1)
                dve.tensor_tensor(prod_lo[:, t % 2, :], prod[:, t % 2, :], prod_hi[:, t % 2, :].bitcast(F32),
                                  ALU.subtract).then_inc(prodl_ready, 1)

            def x0_low(L):
                dve.wait_ge(x0h_ready, L + 1)
                dve.tensor_tensor(x0_split[LOW:LOW + M, :], ps_s[0][0:M, :], x0_split[0:M, :].bitcast(F32),
                                  ALU.subtract).then_inc(x0l_ready, 1)

            def x1_low(L, j0, j1):
                dve.wait_ge(x1h_ready, L * DG + j1)
                cs = slice(j0 * P, j1 * P)
                dve.tensor_tensor(x1_lo[:, cs], x1_sb[:, cs], x1_hi[:, cs].bitcast(F32),
                                  ALU.subtract).then_inc(x1l_ready, j1 - j0)

            def z0_sum(L, dq):
                dve.wait_ge(x1_ready, L + 1)
                dve.tensor_reduce(z0_part[:, dq, :], x1_sb[:].rearrange("h (d b) -> h b d", d=DG),
                                  AX.X, ALU.add).then_inc(z0_parts, 1)

            def z0_total(t):
                dve.wait_ge(h1_full, t)
                dve.wait_ge(z0_parts, (t + 1) * GROUPS)
                dve.tensor_reduce(z0_sb[:], z0_part[:].rearrange("h q b -> h b q"), AX.X,
                                  ALU.add).then_inc(z0_ready, 1)

            def iteration(bt, more):
                for dq in range(GROUPS):
                    g = bt * GROUPS + dq
                    L, dq1 = g + 1, (dq + 1) % GROUPS
                    ahead = more or dq < GROUPS - 1
                    dve.wait_ge(scal_ready, g + 1)
                    for j in range(DG):
                        for e in range(NE):
                            a = j * NE + e
                            macs(g, dq, j, e)
                            if a == 1:
                                x1_low(g, DG - 1, DG)
                            if ahead and a % 2 == 1 and a < 2 * NPAIR:
                                product(L, a // 2)
                            if ahead and a % 2 == 0 and 1 <= a // 2 <= NPAIR:
                                product_low(L, a // 2 - 1)
                            if e == 1 and j > 0:
                                reduce_x2(g, dq, j - 1)
                            if e == 1 and j == 0 and not (isinstance(g, int) and g == 0):
                                reduce_x2(g - 1, (dq - 1) % GROUPS, DG - 1)
                            if a == 16 and dq == GROUPS - 1:
                                z0_total(bt)
                            if a == 17 and ahead:
                                if dq1 == 0:
                                    dve.wait_ge(z0_ready, bt + 1)
                                z0_sum(L, dq1)
                                x1_low(L, 0, DG - 1)
                            if a == 18 and (more or dq < GROUPS - 2):
                                x0_low(L + 1)

            dve.memset(x0_split[:].bitcast(F32), 0.0).then_inc(split_zeroed, 1)
            dve.memset(blocks[:], 0.0).then_inc(blocks_zeroed, 1)
            dve.wait_ge(small_in, 16 * 5)
            dve.tensor_tensor(pairs, pairs, pairs_b, ALU.add).then_inc(pairs_ready, 1)
            dve.wait_ge(blocks_zeroed, 1)
            dve.tensor_copy(blocks[:, :, KB * M:GW], mask[:].unsqueeze(1).to_broadcast([P, NK, KB])).then_inc(blocks_init, 1)
            dve.wait_ge(k1h_ready, 1)
            dve.tensor_tensor(k1_lo[:], k1_stage, k1_hi[:].bitcast(F32), ALU.subtract).then_inc(k1l_ready, 1)
            dve.wait_ge(halves_ready, 2)
            dve.tensor_tensor(pairs_lo[:], pairs, pairs_hi[:].bitcast(F32), ALU.subtract).then_inc(halves_ready, 1)
            x0_low(0)
            product(0, 0)
            for t in range(NPAIR):
                if t + 1 < NPAIR:
                    product(0, t + 1)
                product_low(0, t)
            x0_low(1)
            z0_sum(0, 0)
            x1_low(0, 0, DG - 1)
            iteration(0, True)
            with dve.Fori(1, BT - 1) as bt:
                iteration(bt, True)
            iteration(BT - 1, False)
            reduce_x2(BT * GROUPS - 1, GROUPS - 1, DG - 1)

        @block.scalar
        def _(act):
            def scale_bank(g, dq, j, a):
                e = a - j * NE
                tile = g * DG + j
                act.wait_ge(ya_full, g * (DG * NE) + a + 1)
                if not (isinstance(g, int) and g * DG + j < 2):
                    act.wait_ge(pool_added, (tile - 1) * (NE - 1))
                y = ps_ya[a % 2]
                for i in range(MB):
                    m = (2 * e + 1) * MB + i
                    at = e * COLS + i * H
                    ins = act.activation(scaled[:, j % 2, at:at + H], y[:, i * H:(i + 1) * H], ACT.Copy,
                                         scale=scalar_of(m, dq * DG + j))
                ins.then_inc(scaled_ready, 1)

            def x0_out(L, t, dq):
                act.wait_ge(x0_full, L + 1)
                act.wait_ge(shift_full, L * NPAIR)
                act.activation(x0_split[0:M, :], ps_s[0][0:M, :], ACT.Copy)
                if dq == 0:
                    act.wait_ge(x0g_full, 2 * t)
                act.activation(x0t_v[:, dq * DG:(dq + 1) * DG, :],
                               ps_s[0][0:M, :].rearrange("m (d b) -> m d b", d=DG), ACT.Copy).then_inc(x0h_ready, 1)

            def replicas_out(L):
                act.wait_ge(rep_full, L + 1)
                act.wait_ge(prod_ready, L * NPAIR)
                act.activation(x0_rep[:], ps_s[0][0:ROWS, :], ACT.Copy).then_inc(rep_ready, 1)

            def product_high(L, t):
                n = L * NPAIR + t
                act.wait_ge(prod_ready, n + 1)
                if t < 2:
                    act.wait_ge(pair_mm, L * NPAIR)
                else:
                    act.wait_ge(pair_mm, n - 1)
                act.activation(prod_hi[:, t % 2, :], prod[:, t % 2, :], ACT.Copy).then_inc(prodh_ready, 1)

            def x1_out(L):
                act.wait_ge(pair_mm, (L + 1) * NPAIR)
                act.wait_ge(z0_parts, L)
                act.wait_ge(x1l_ready, L * DG)
                act.activation(x1_sb[:], ps_x1[:], ACT.Copy).then_inc(x1_ready, 1)

            def x1_high(L, j0, j1):
                act.wait_ge(x1_ready, L + 1)
                if not (isinstance(L, int) and L == 0):
                    act.wait_ge(ya_full, (L - 1) * (DG * NE) + j1 * NE)
                cs = slice(j0 * P, j1 * P)
                act.activation(x1_hi[:, cs], x1_sb[:, cs], ACT.Copy).then_inc(x1h_ready, j1 - j0)

            def take_embeddings(t):
                act.wait_ge(gathered, (t + 1) * M * 16)
                act.wait_ge(x0_full, t * GROUPS)
                act.wait_ge(scal_ready, t * GROUPS)
                act.activation(emb[:], emb_raw[:], ACT.Copy).then_inc(emb_ready, 1)

            def take_scalars(t, dq):
                act.wait_ge(emb_ready, t + 1)
                if not (isinstance(t, int) and t == 0):
                    act.wait_ge(mac_done, ((t - 1) * GROUPS + dq + 1) * DG * MACS)
                ds = slice(dq * DG, (dq + 1) * DG)
                act.activation(sc_v[:, :, ds], emb_v[:, 0:M, ds], ACT.Copy).then_inc(scal_ready, 1)

            def x0g_out(bt, half):
                act.wait_ge(x0g_full, 2 * bt + half + 1)
                act.wait_ge(blocks_in, 16 * KB * bt)
                w = NK // 2 * M
                act.activation(x0_g[:, half * w:(half + 1) * w], ps_tail[:, 0:w], ACT.Copy).then_inc(x0g_ready, 1)

            def gram_out(t, k, banks=(ps_tail,)):
                act.wait_ge(gram_full, t * NK + k + 1)
                act.activation(gram[:, k, :], banks[k % len(banks)][:, 0:GW], ACT.Copy).then_inc(gram_ready, 1)

            def z2_out(t):
                act.wait_ge(z2_full, t + 1)
                act.activation(z2_sb, ps_tail[:, 0:P], ACT.Copy).then_inc(z2_ready, 1)

            def relu(t, full, ready, dst, bias, n):
                act.wait_ge(full, t + 1)
                for o in range(n):
                    ins = act.activation(dst[:, o, :], ps_tail[:, o * P:(o + 1) * P], ACT.Relu, bias=bias[:, o:o + 1])
                ins.then_inc(ready, 1)

            def y_out(t):
                act.wait_ge(y_full, t + 1)
                act.activation(y_sb, ps_tail[0:1, 0:P], ACT.Copy).then_inc(y_ready, 1)

            def iteration(bt, tail, more):
                for dq in range(GROUPS):
                    g = bt * GROUPS + dq
                    L, dq1 = g + 1, (dq + 1) % GROUPS
                    ahead = more or dq < GROUPS - 1
                    if dq == 0 and more:
                        act.dma_start(idx[:], ids[bass.ds((bt + 1) * P, P), :]).then_inc(idx_in, 16)
                    for j in range(DG):
                        for e in range(NE):
                            a = j * NE + e
                            if a == 0:
                                act.wait_ge(scal_ready, g + 1)
                            scale_bank(g, dq, j, a)
                            if a == 0:
                                x1_high(g, DG - 1, DG)
                            if a == 0 and ahead:
                                replicas_out(L)
                            if ahead and a % 2 == 1 and a < 2 * NPAIR:
                                product_high(L, a // 2)
                            if a == 14 and dq == 2 and more:
                                take_embeddings(bt + 1)
                            if a == 6 and dq == 3 and more:
                                for s in range(3):
                                    take_scalars(bt + 1, s)
                            if a == 6 and dq == 0:
                                if tail:
                                    take_scalars(bt, 3)
                            if tail and dq == 1 and 1 <= a < 1 + NK:
                                gram_out(bt - 1, a - 1)
                            if dq == 2 and a in (2, 4):
                                x0g_out(bt, a // 2 - 1)
                            if tail and dq == 2 and a == 16:
                                z2_out(bt - 1)
                            if tail and dq == 3 and a == 6:
                                relu(bt - 1, h1_full, h1_ready, h1_sb, b1_sb, O1)
                            if tail and dq == 3 and a == 10:
                                relu(bt - 1, h2_full, h2_ready, h2_sb, b2_sb, O2)
                            if tail and dq == 3 and a == 13:
                                y_out(bt - 1)
                            if a == 16 and ahead:
                                x1_out(L)
                                x1_high(L, 0, DG - 1)
                            if a == 17 and (more or dq < GROUPS - 2):
                                x0_out(L + 1, bt + (dq + 2) // GROUPS, (dq + 2) % GROUPS)

            act.wait_ge(small_in, 16 * 5)
            act.activation(select[:], select_stage, ACT.Copy).then_inc(halves_ready, 1)
            act.wait_ge(pairs_ready, 1)
            act.activation(pairs_hi[:], pairs, ACT.Copy).then_inc(halves_ready, 1)
            act.wait_ge(k1_in, 16)
            act.activation(k1_hi[:], k1_stage, ACT.Copy).then_inc(k1h_ready, 1)
            take_embeddings(0)
            for s in range(GROUPS):
                take_scalars(0, s)
            act.wait_ge(split_zeroed, 1)
            x0_out(0, 0, 0)
            replicas_out(0)
            for t in range(NPAIR):
                product_high(0, t)
            x0_out(1, 0, 1)
            x1_out(0)
            x1_high(0, 0, DG - 1)
            act.wait_ge(k1l_ready, 1)
            act.wait_ge(late_in, 16 * 7)
            iteration(0, False, True)
            with act.Fori(1, BT - 1) as bt:
                iteration(bt, True, True)
            iteration(BT - 1, True, False)
            t = BT - 1
            for k in range(NK):
                gram_out(t, k, last_banks)
            z2_out(t)
            relu(t, h1_full, h1_ready, h1_sb, b1_sb, O1)
            relu(t, h2_full, h2_ready, h2_sb, b2_sb, O2)
            y_out(t)

        @block.gpsimd
        def _(pool):
            def gather(t, f):
                if f == 0:
                    pool.wait_ge(idx_in, 16 * (t + 1))
                    pool.nop(nofuse=True)
                    pool.wait_ge(emb_ready, t)
                    pool.nop(nofuse=True)
                pool.indirect_dma_start(emb_raw[:, f * D:(f + 1) * D], None, tables[f],
                                        bass.IndirectOffsetOnAxis(ap=idx[:, f:f + 1], axis=0)).then_inc(gathered, 16)

            def iteration(bt, more):
                for dq in range(GROUPS):
                    g = bt * GROUPS + dq
                    for j in range(DG):
                        tile = g * DG + j
                        dst = sums[:, j % 2, MB:2 * MB, :].rearrange("p s o -> p (s o)")
                        for e in range(1, NE):
                            pool.wait_ge(scaled_ready, g * (DG * NE) + j * NE + e + 1)
                            src = scaled[:, j % 2, e * COLS:(e + 1) * COLS]
                            if e == 1:
                                if not (isinstance(g, int) and g * DG + j < 2):
                                    pool.wait_ge(x2_ready, tile - 1)
                                other = scaled[:, j % 2, 0:COLS]
                            else:
                                pool.wait_ge(pool_added, tile * (NE - 1) + e - 1)
                                other = dst
                            pool.tensor_tensor(dst, src, other, ALU.add).then_inc(pool_added, 1)
                            slot = j * (NE - 1) + e - 1
                            f = dq * 15 + slot - 1
                            if more and dq < 3 and 1 <= slot and f < min(M, 15 * (dq + 1)):
                                gather(bt + 1, f)

            for f in range(M):
                gather(0, f)
            iteration(0, True)
            with pool.Fori(1, BT - 1) as bt:
                iteration(bt, True)
            iteration(BT - 1, False)


def select_rows(np):
    i, j = np.tile(np.arange(M), SH), np.repeat(np.arange(SH), M)
    fields = np.concatenate([(i - NPAIR * j) % M] + [(i + t) % M for t in range(NPAIR)])
    out = np.zeros((LOW + M, fields.size), np.float32)
    for at in (0, LOW):
        out[at + fields, np.arange(fields.size)] = 1.0
    return out


def kernel(**inputs):
    import numpy as np
    from concourse import bacc
    from concourse.bass_utils import run_bass_kernel_spmd

    a = {k: np.asarray(v) for k, v in inputs.items()}
    k0 = a["L0_rec_k0"]
    i, j = np.tile(np.arange(M), SH), np.repeat(np.arange(SH), M)
    h = (i - NPAIR * j) % M
    lay_a, lay_b = [], []
    for t in range(NPAIR):
        shift, m = NPAIR * j + t, (i + t) % M
        lay_a.append(k0[:, h, m].T)
        twice = np.isin(shift, (0, M // 2))
        lay_b.append(np.where(twice[:, None], np.zeros((), k0.dtype), k0[:, m, h].T))
    arrays = {
        "ids": a["ids"],
        "dense_t": np.ascontiguousarray(a["dense_ctx"].T),
        "k0a": np.ascontiguousarray(np.concatenate(lay_a, axis=1)),
        "k0b": np.ascontiguousarray(np.concatenate(lay_b, axis=1)),
        "k1": np.ascontiguousarray(a["L0_rec_k1"].transpose(1, 2, 0)).reshape(H, M * H),
        "k2": np.ascontiguousarray(a["L0_rec_k2"].transpose(1, 2, 0)).reshape(H, M * H),
        "w1": np.ascontiguousarray(a["W_top1"][:3 * P].reshape(3, P, F1).transpose(1, 0, 2)),
        "w1d": np.ascontiguousarray(a["W_top1"][3 * P:]),
        "b1": np.ascontiguousarray(a["b_top1"].reshape(O1, P).T),
        "w2": np.ascontiguousarray(a["W_top2"].reshape(O1, P, F2).transpose(1, 0, 2)),
        "b2": np.ascontiguousarray(a["b_top2"].reshape(O2, P).T),
        "w3": np.ascontiguousarray(a["W_top3"].reshape(O2, P).T),
        "ident_in": np.eye(P, dtype=np.float32),
        "select_in": select_rows(np),
        "mask_in": np.kron(np.eye(KB, dtype=np.float32), np.ones((D, 1), np.float32)),
    }
    tables = {f"tbl_{f}": a[f"tbl_{f}"] for f in range(M)}
    nc = bacc.Bacc("TRN2", target_bir_lowering=False, num_devices=1)

    def dram(name, array):
        return nc.dram_tensor(name, array.shape, mybir.dt.from_np(array.dtype), kind="ExternalInput").ap()

    args = {name: dram(name, array) for name, array in arrays.items()}
    tabs = [dram(name, array) for name, array in tables.items()]
    out = nc.dram_tensor("out", [B, 1], F32, kind="ExternalOutput").ap()
    build(nc, tables=tabs, out=out, **args)
    r = run_bass_kernel_spmd(nc, [{**arrays, **tables}], core_ids=[0])
    return r.results[0]["out"]
```

```python
from contextlib import ExitStack

import concourse.bass as bass
from concourse import mybir

B, M, D, H = 512, 40, 16, 128
P = 128
BT = B // P
KB = P // D
NK = P // KB
DG = 4
GROUPS = NK // DG
COLS = DG * P
GB = DG * KB
SH = 3
EXT = P
ROWS = SH * M
SLOTS = 4
NPAIR = (M // 2 + 1) // SH
MB = COLS // H
NB = M // MB
NQ = DG * NB
WARM_UP = 14
YR = 5
READERS = ("SVSVSVSVSV", "SVSSVSSVSV")
OWNER = "".join(READERS[j % 2] for j in range(DG))
RANK = [OWNER[:q].count(OWNER[q]) for q in range(NQ)]
V_AT = [OWNER[:NB * j].count("V") for j in range(DG + 1)]
S_AT = [OWNER[:NB * j].count("S") for j in range(DG + 1)]
ADD_AT = [S_AT[j] - j for j in range(DG + 1)]
NV, NS, NADD = V_AT[DG], S_AT[DG], ADD_AT[DG]
PROD_Q = (3, 6, 9, 12, 16, 19, 22)
HIGH_Q = tuple(q + 3 for q in PROD_Q)
LOW_Q = tuple(q + 4 for q in PROD_Q)
PAIR_Q = tuple(q + 9 for q in PROD_Q)
PR = 3
HR = 3
X0_BLOCKS_Q = (4, 34, 1, 18)
GRAM_Q = ((), (), (6, 10, 14, 18, 23, 27, 32, 37), (3, 7, 11, 15, 23, 31, 37))
FIRST_K = (0, 0, 0, len(GRAM_Q[2]))
LAST_GRAM_Q = 9
LAYER2_Q, LAYER2_STEPS = 12, 24
MLP1_Q, MLP2_Q, MLP3_Q = (3, 5, 7, 8), (15, 17), 23
EXTEND_Q = 25
X0_COLS_Q = (28, 30, 33, 35)
X0_OUT_Q = (27, 29, 32, 34)
SR = next(r for r in range(6, NADD + 1) if NADD % r == 0)
REDUCE_Q = 6
GATHER_AT = (0, 12, 22, 33, M)
GW = KB * M + KB
F1, F2 = 512, 256
ND = 16
O1, O2 = F1 // P, F2 // P

F32 = mybir.dt.float32
F32R = mybir.dt.float32r
I32 = mybir.dt.int32
ALU = mybir.AluOpType
ACT = mybir.ActivationFunctionType
AX = mybir.AxisListType


def build(nc, ids, tables, dense_t, k0a, k0b, k1, k2, w1, w1d, b1, w2, b2, w3, ident_in, mask_in, out):
    with ExitStack() as ctx:
        def sb(name, shape, dt=F32):
            return ctx.enter_context(nc.sbuf_tensor(name, shape, dt))

        def sem(name):
            return ctx.enter_context(nc.semaphore(name))

        pairs_hi = sb("pairs_hi", [ROWS, NPAIR * H], F32R)
        pairs_lo = sb("pairs_lo", [ROWS, NPAIR * H], F32R)
        k1_hi = sb("k1_hi", [H, M * H], F32R)
        k1_lo = sb("k1_lo", [H, M * H], F32R)
        k2_sb = sb("k2_sb", [H, M * H])
        w1_sb = sb("w1_sb", [P, 3, F1])
        w2_sb = sb("w2_sb", [P, O1, F2])
        w3_sb = sb("w3_sb", [P, O2])
        b1_sb = sb("b1_sb", [P, O1])
        b2_sb = sb("b2_sb", [P, O2])
        ident = sb("ident", [P, P])
        mask = sb("mask", [P, KB])
        idx = sb("idx", [P, M], I32)
        emb = sb("emb", [P, EXT * D])
        x0_g = sb("x0_g", [P, NK, M])
        x0_t = sb("x0_t", [EXT, P * D])
        first = sb("first", [ROWS, COLS])
        second = sb("second", [ROWS, SLOTS, COLS])
        prod = sb("prod", [ROWS, PR, COLS])
        prod_hi = sb("prod_hi", [ROWS, HR, COLS], F32R)
        prod_lo = sb("prod_lo", [ROWS, HR, COLS], F32R)
        x1_sb = sb("x1_sb", [H, COLS])
        x1_hi = sb("x1_hi", [H, COLS], F32R)
        x1_lo = sb("x1_lo", [H, COLS], F32R)
        z0_sb = sb("z0_sb", [H, P])
        z0_mlp = sb("z0_mlp", [H, P])
        scaled = sb("scaled", [P, SR, COLS])
        sums = sb("sums", [P, DG, 2 * MB, H])
        warm_up_mark = sb("warm_up_mark", [1, 1])
        x2_k = sb("x2_k", [P, NK, H])
        blocks = sb("blocks", [P, 2, DG, GW])
        gram = sb("gram", [H, NK, GW])
        z1_sb = sb("z1_sb", [H, P])
        z2_sb = sb("z2_sb", [H, P])
        h1_sb = sb("h1_sb", [P, O1, P])
        h2_sb = sb("h2_sb", [P, O2, P])
        y_sb = sb("y_sb", [1, P])
        w1d_sb = sb("w1d_sb", [ND, F1])
        dense_sb = sb("dense_sb", [ND, P])
        pairs_b = prod[:].rearrange("p a c -> p (a c)")[:, 0:NPAIR * H]
        scaled_flat = scaled[:].rearrange("p a c -> p (a c)")
        pairs = scaled_flat[0:ROWS, 0:NPAIR * H]
        k1_stage = gram[:].rearrange("h k w -> h (k w)")[:, 0:M * H]

        ps = [ctx.enter_context(nc.psum_tensor(n, [P, COLS], F32))
              for n in ("ps_y0", "ps_y1", "ps_y2", "ps_y3", "ps_y4", "ps_s", "ps_x1", "ps_tail")]
        ps_y, ps_s, ps_x1, ps_tail = ps[0:YR], ps[YR], ps[YR + 1], ps[YR + 2]

        idx_in = sem("idx_in")
        small_in = sem("small_in")
        k1_in = sem("k1_in")
        late_in = sem("late_in")
        gathered = sem("gathered")
        gathers_near_end = sem("gathers_near_end")
        pairs_ready = sem("pairs_ready")
        halves_ready = sem("halves_ready")
        k1h_ready = sem("k1h_ready")
        k1l_ready = sem("k1l_ready")
        blocks_zeroed = sem("blocks_zeroed")
        blocks_init = sem("blocks_init")
        emb_ready = sem("emb_ready")
        x0_full = sem("x0_full")
        x0t_ready = sem("x0t_ready")
        first_in = sem("first_in")
        second_in = [sem(f"second_in{i}") for i in range(SLOTS)]
        prod_ready = sem("prod_ready")
        prodh_ready = sem("prodh_ready")
        prodl_ready = sem("prodl_ready")
        pair_mm = sem("pair_mm")
        x1_ready = sem("x1_ready")
        x1h_ready = sem("x1h_ready")
        x1l_ready = sem("x1l_ready")
        yv_full = sem("yv_full")
        ys_full = sem("ys_full")
        mac_done = sem("mac_done")
        scaled_ready = sem("scaled_ready")
        pool_added = sem("pool_added")
        x2_ready = sem("x2_ready")
        x0g_full = sem("x0g_full")
        x0g_ready = sem("x0g_ready")
        blocks_in = (sem("even_blocks_in"), sem("odd_blocks_in"))
        gram_full = sem("gram_full")
        gram_ready = sem("gram_ready")
        z0_ready = sem("z0_ready")
        z0_copied = sem("z0_copied")
        z1_ready = sem("z1_ready")
        z2_full = sem("z2_full")
        z2_ready = sem("z2_ready")
        dense_in = sem("dense_in")
        h1_full = sem("h1_full")
        h1_ready = sem("h1_ready")
        h2_full = sem("h2_full")
        h2_ready = sem("h2_ready")
        y_full = sem("y_full")
        y_ready = sem("y_ready")
        y_stored = sem("y_stored")

        emb_v = emb[:].rearrange("p (m d) -> p m d", d=D)
        gram_v = gram[:, :, 0:KB * M].rearrange("h k (b m) -> h k b m", b=KB)
        x0t_v = x0_t[:].rearrange("m (k d b) -> m d k b", k=NK, d=D)
        out_v = out.rearrange("(t b) o -> t (o b)", t=BT)

        ps_first = (ps_s, *ps_y[0:3])

        ps_h1 = (ps_x1, ps_s, *ps_y[0:2])

        block = ctx.enter_context(nc.Block())

        @block.sync
        def _(sp):
            for dst, src in ((ident, ident_in), (mask, mask_in)):
                sp.dma_start(dst[:], src).then_inc(small_in, 16)
            for dst, src in ((pairs, k0a), (pairs_b, k0b)):
                sp.dma_start(dst, src).then_inc(small_in, 16)
            sp.dma_start(k1_stage, k1).then_inc(k1_in, 16)
            for dst, src in ((k2_sb, k2), (w1_sb, w1), (w2_sb, w2), (w3_sb, w3),
                             (b1_sb, b1), (b2_sb, b2)):
                sp.dma_start(dst[:], src).then_inc(late_in, 16)
            sp.dma_start(w1d_sb[:], w1d).then_inc(late_in, 16)

            def load_first(L, dq):
                if not (isinstance(L, int) and L == 0):
                    sp.wait_ge(prod_ready, L * NPAIR)
                    sp.nop(nofuse=True)
                for j in range(SH):
                    sp.dma_start(first[j * M:(j + 1) * M, :],
                                 x0_t[M - NPAIR * j:2 * M - NPAIR * j, dq * COLS:(dq + 1) * COLS]).then_inc(first_in, 16)

            def load_second(L, dq, t):
                if t >= SLOTS:
                    sp.wait_ge(prod_ready, L * NPAIR + t - SLOTS + 1)
                    sp.nop(nofuse=True)
                elif not (isinstance(L, int) and L == 0):
                    sp.wait_ge(prod_ready, (L - 1) * NPAIR + t + (NPAIR - 1 - t) // SLOTS * SLOTS + 1)
                    sp.nop(nofuse=True)
                sp.dma_start(second[:, t % SLOTS, :],
                             x0_t[t:t + ROWS, dq * COLS:(dq + 1) * COLS]).then_inc(second_in[t % SLOTS], 16)

            def lay_blocks(g, dq):
                sp.wait_ge(x0g_ready, g + 1)
                sp.nop(nofuse=True)
                if isinstance(g, int) and g < 2:
                    sp.wait_ge(blocks_init, 1)
                else:
                    sp.wait_ge(gram_full, (g - 1) * DG)
                    sp.nop(nofuse=True)
                xv = x0_g[:, dq * DG:(dq + 1) * DG, :]
                for i in range(KB):
                    rows = slice(i, P, KB)
                    sp.dma_start(blocks[rows, dq % 2, :, i * M:(i + 1) * M], xv[rows]).then_inc(blocks_in[dq % 2], 16)

            def load_dense(t):
                sp.dma_start(dense_sb[:], dense_t[:, bass.ds(t * P, P)]).then_inc(dense_in, 16)

            def store_y(t):
                sp.wait_ge(y_ready, t + 1)
                sp.nop(nofuse=True)
                sp.dma_start(out_v[bass.ds(t, 1), :], y_sb[:]).then_inc(y_stored, 16)
                sp.wait_ge(y_stored, 16 * (t + 1))
                sp.nop(nofuse=True)

            def iteration(bt, tail, more):
                for dq in range(GROUPS):
                    g = bt * GROUPS + dq
                    if more or dq < GROUPS - 1:
                        for t in range(SLOTS, NPAIR):
                            load_second(g + 1, (dq + 1) % GROUPS, t)
                    if dq == 0:
                        lay_blocks(bt * GROUPS, 0)
                        lay_blocks(bt * GROUPS + 1, 1)
                    elif dq >= 2:
                        lay_blocks(bt * GROUPS + dq, dq)
                    if more or dq < GROUPS - 2:
                        if dq == 2:
                            sp.wait_ge(x0t_ready, (bt + 2) * GROUPS)
                            sp.nop(nofuse=True)
                        for t in range(SLOTS):
                            load_second(g + 2, (dq + 2) % GROUPS, t)
                        load_first(g + 2, (dq + 2) % GROUPS)
                    if dq == 1:
                        if tail:
                            store_y(bt - 1)
                        load_dense(bt)

            sp.wait_ge(x0t_ready, GROUPS)
            load_first(0, 0)
            for t in range(NPAIR):
                load_second(0, 0, t)
            for t in range(SLOTS):
                load_second(1, 1, t)
            load_first(1, 1)
            iteration(0, False, True)
            with sp.Fori(1, BT - 1) as bt:
                iteration(bt, True, True)
            iteration(BT - 1, True, False)
            store_y(BT - 1)

        @block.tensor
        def _(pe):
            def x0_columns(t, c, banks=(ps_s,)):
                if c == 0:
                    pe.wait_ge(emb_ready, t + 1)
                    pe.nop(nofuse=True)
                if c >= len(banks) or c == 0 and not (isinstance(t, int) and t == 0):
                    pe.wait_ge(x0t_ready, t * GROUPS + max(c - len(banks) + 1, 0))
                    pe.nop(nofuse=True)
                for i in range(D // GROUPS):
                    ins = pe.transpose(banks[c % len(banks)][:, i * P:(i + 1) * P], emb_v[:, :, c * (D // GROUPS) + i],
                                       ident[:])
                ins.then_inc(x0_full, 1)

            def pair_matmul(L, t):
                if t == 0:
                    pe.wait_ge(x1_ready, L)
                pe.wait_ge(prodl_ready, L * NPAIR + t + 1)
                ks = slice(t * H, (t + 1) * H)
                pe.matmul(ps_x1[:], pairs_hi[:, ks], prod_hi[:, t % HR, :], start=(t == 0), stop=False)
                pe.matmul(ps_x1[:], pairs_lo[:, ks], prod_hi[:, t % HR, :], start=False, stop=False)
                pe.matmul(ps_x1[:], pairs_hi[:, ks], prod_lo[:, t % HR, :],
                          start=False, stop=(t == NPAIR - 1)).then_inc(pair_mm, 1)

            def bank(g, q):
                j, n, e = q // NB, q % NB, RANK[q]
                if n == 0:
                    pe.wait_ge(x1l_ready, g * DG + j + 1)
                before = RANK[q - YR] + 1
                if q >= YR and OWNER[q - YR] == "V":
                    pe.wait_ge(mac_done, (g * NV + before) * MB)
                elif q >= YR:
                    pe.wait_ge(scaled_ready, g * NS + before)
                elif isinstance(g, int) and g == 0:
                    if q == 0:
                        pe.wait_ge(x0t_ready, GROUPS)
                elif OWNER[q - YR] == "V":
                    pe.wait_ge(mac_done, ((g - 1) * NV + before) * MB)
                else:
                    pe.wait_ge(scaled_ready, (g - 1) * NS + before)
                y, full = ps_y[q % YR], yv_full if OWNER[q] == "V" else ys_full
                hi, lo = x1_hi[:, j * P:(j + 1) * P], x1_lo[:, j * P:(j + 1) * P]
                ks = slice(n * COLS, (n + 1) * COLS)
                pe.matmul(y[:], hi, k1_hi[:, ks], start=True, stop=False)
                pe.matmul(y[:], hi, k1_lo[:, ks], start=False, stop=False)
                pe.matmul(y[:], lo, k1_hi[:, ks], start=False, stop=True).then_inc(full, 1)

            def gram_block(t, k):
                n = t * NK + k
                pe.wait_ge(x2_ready, n + 1)
                if k % DG == 0:
                    pe.wait_ge(blocks_in[k // DG % 2], 16 * KB * (t * (GROUPS // 2) + k // DG // 2 + 1))
                if not (isinstance(n, int) and n == 0):
                    pe.wait_ge(gram_ready, n)
                pe.matmul(ps_tail[:, 0:GW], x2_k[:, k, :], blocks[:, k // DG % 2, k % DG, :],
                          start=True, stop=True).then_inc(gram_full, 1)

            def x0_blocks(g, t, dq):
                if dq == 0:
                    pe.wait_ge(x0t_ready, (t + 1) * GROUPS)
                    pe.nop(nofuse=True)
                for j in range(DG):
                    k = dq * DG + j
                    ins = pe.transpose(ps_tail[:, j * M:(j + 1) * M], x0_t[0:M, k * P:(k + 1) * P], ident[0:M, 0:M])
                ins.then_inc(x0g_full, 1)

            def layer2(t, m0, m1):
                if m0 == 0:
                    pe.wait_ge(gram_ready, (t + 1) * NK)
                for m in range(m0, m1):
                    ins = pe.matmul(ps_tail[:, 0:P].rearrange("o (k b) -> o k b", k=NK), k2_sb[:, m * H:(m + 1) * H],
                                    gram_v[:, :, :, m], start=(m == 0), stop=(m == M - 1))
                if m1 == M:
                    ins.then_inc(z2_full, 1)

            def mlp1_begin(t, o, dst):
                if o == 0:
                    pe.wait_ge(z0_copied, t + 1)
                    pe.wait_ge(dense_in, 16 * (t + 1))
                fs = slice(o * P, (o + 1) * P)
                pe.matmul(dst, w1_sb[:, 0, fs], z0_mlp[:], start=True, stop=False)
                pe.matmul(dst, w1d_sb[:, fs], dense_sb[:], start=False, stop=False)

            def mlp1_z1(t, o, dst):
                if o == 0:
                    pe.wait_ge(z1_ready, t + 1)
                pe.matmul(dst, w1_sb[:, 1, o * P:(o + 1) * P], z1_sb[:], start=False, stop=False)

            def mlp1_z2(t, o, dst):
                if o == 0:
                    pe.wait_ge(z2_ready, t + 1)
                ins = pe.matmul(dst, w1_sb[:, 2, o * P:(o + 1) * P], z2_sb[:], start=False, stop=True)
                if o == O1 - 1:
                    ins.then_inc(h1_full, 1)

            def mlp1(t, o):
                dst = ps_tail[:, o * P:(o + 1) * P]
                if o == 0:
                    pe.wait_ge(z2_ready, t + 1)
                mlp1_begin(t, o, dst)
                mlp1_z1(t, o, dst)
                mlp1_z2(t, o, dst)

            def mlp2(t, o):
                if o == 0:
                    pe.wait_ge(h1_ready, t + 1)
                for i in range(O1):
                    ins = pe.matmul(ps_tail[:, o * P:(o + 1) * P], w2_sb[:, i, o * P:(o + 1) * P],
                                    h1_sb[:, i, :], start=(i == 0), stop=(i == O1 - 1))
                if o == O2 - 1:
                    ins.then_inc(h2_full, 1)

            def mlp3(t):
                pe.wait_ge(h2_ready, t + 1)
                for i in range(O2):
                    ins = pe.matmul(ps_tail[0:1, 0:P], w3_sb[:, i:i + 1], h2_sb[:, i, :],
                                    start=(i == 0), stop=(i == O2 - 1))
                ins.then_inc(y_full, 1)

            def iteration(bt, tail, more):
                for dq in range(GROUPS):
                    g = bt * GROUPS + dq
                    L = g + 1
                    ahead = more or dq < GROUPS - 1
                    for q in range(NQ):
                        bank(g, q)
                        if ahead and q in PAIR_Q:
                            pair_matmul(L, PAIR_Q.index(q))
                        if more and dq == GROUPS - 2 and q in X0_COLS_Q:
                            x0_columns(bt + 1, X0_COLS_Q.index(q))
                        if ahead and q == X0_BLOCKS_Q[dq]:
                            if dq == 0:
                                if tail:
                                    pe.wait_ge(gram_ready, bt * NK - 1)
                                else:
                                    pe.wait_ge(x0g_ready, 1)
                            elif dq == 1:
                                if tail:
                                    pe.wait_ge(y_ready, bt)
                                else:
                                    pe.wait_ge(x0g_ready, g + 1)
                            elif dq == 2:
                                pe.wait_ge(x0g_ready, g + 1)
                            else:
                                pe.wait_ge(gram_ready, bt * NK + FIRST_K[dq] + sum(p < q for p in GRAM_Q[dq]))
                            pe.nop(nofuse=True)
                            x0_blocks(L, bt + (dq + 1) // GROUPS, (dq + 1) % GROUPS)
                        if tail and dq == 0 and q == LAST_GRAM_Q:
                            pe.wait_ge(x0g_ready, g + 2)
                            gram_block(bt - 1, NK - 1)
                        if q in GRAM_Q[dq]:
                            if ahead and q == min(p for p in GRAM_Q[dq] if p > X0_BLOCKS_Q[dq]):
                                pe.wait_ge(x0g_ready, g + 2)
                            gram_block(bt, FIRST_K[dq] + GRAM_Q[dq].index(q))
                        if tail and dq == 0 and 0 <= q - LAYER2_Q < LAYER2_STEPS:
                            a = q - LAYER2_Q
                            layer2(bt - 1, a * M // LAYER2_STEPS, (a + 1) * M // LAYER2_STEPS)
                        if tail and dq == 1 and q in MLP1_Q:
                            mlp1(bt - 1, MLP1_Q.index(q))
                        if tail and dq == 1 and q in MLP2_Q:
                            mlp2(bt - 1, MLP2_Q.index(q))
                        if tail and dq == 1 and q == MLP3_Q:
                            mlp3(bt - 1)

            pe.wait_ge(small_in, 16 * 4)
            pe.wait_ge(halves_ready, 2)
            pe.wait_ge(gathers_near_end, 1)
            for _ in range(WARM_UP):
                pe.matmul(ps_tail[:], pairs_hi[:, 0:H], pairs_hi[:, 0:COLS], start=True, stop=True)
            for c in range(GROUPS):
                x0_columns(0, c, ps_first)
            x0_blocks(0, 0, 0)
            for t in range(NPAIR):
                pair_matmul(0, t)
            pe.wait_ge(k1l_ready, 1)
            iteration(0, False, True)
            pe.wait_ge(late_in, 16 * 7)
            with pe.Fori(1, BT - 1) as bt:
                iteration(bt, True, True)
            iteration(BT - 1, True, False)
            t = BT - 1
            for o in range(O1):
                if o == 2:
                    pe.wait_ge(mac_done, BT * GROUPS * NV * MB)
                    pe.wait_ge(scaled_ready, BT * GROUPS * NS)
                mlp1_begin(t, o, ps_h1[o][:, 0:P])
            gram_block(t, NK - 1)
            layer2(t, 0, M)
            for o in range(O1):
                mlp1_z1(t, o, ps_h1[o][:, 0:P])
            for o in range(O1):
                mlp1_z2(t, o, ps_h1[o][:, 0:P])
            for o in range(O2):
                mlp2(t, o)
            mlp3(t)

        @block.vector
        def _(dve):
            def macs(g, dq, q):
                j, n, e = q // NB, q % NB, RANK[q]
                dve.wait_ge(yv_full, g * NV + e + 1)
                for i in range(MB):
                    acc = sums[:, j, i, :]
                    y = ps_y[q % YR][:, i * H:(i + 1) * H]
                    s = x0_g[:, dq * DG + j, n * MB + i:n * MB + i + 1]
                    if e == V_AT[j]:
                        ins = dve.tensor_scalar(acc, y, s, None, ALU.mult)
                    else:
                        dve.wait_ge(mac_done, (g * NV + e - 1) * MB + i + 1)
                        ins = dve.scalar_tensor_tensor(out=acc, in0=y, scalar=s, in1=acc, op0=ALU.mult, op1=ALU.add)
                    ins.then_inc(mac_done, 1)

            def reduce_x2(g, k):
                j = k % DG
                dve.wait_ge(mac_done, (g * NV + V_AT[j + 1]) * MB)
                dve.wait_ge(pool_added, g * NADD + ADD_AT[j + 1])
                if not (isinstance(g, int) and g < GROUPS):
                    dve.wait_ge(gram_full, (g - GROUPS) * DG + j + (2 if k == NK - 1 else 1))
                dve.tensor_reduce(x2_k[:, k, :], sums[:, j].rearrange("p s o -> p o s"),
                                  AX.X, ALU.add).then_inc(x2_ready, 1)

            def extend_embeddings(t):
                dve.wait_ge(gathered, (t + 1) * M * 16)
                if not (isinstance(t, int) and t == 0):
                    dve.wait_ge(x0_full, t * GROUPS)
                n = EXT // M - 1
                dve.tensor_copy(emb[:, M * D:(n + 1) * M * D].rearrange("p (r f) -> p r f", r=n),
                                emb[:, 0:M * D].unsqueeze(1).to_broadcast([P, n, M * D]))
                dve.tensor_copy(emb[:, (n + 1) * M * D:], emb[:, 0:(EXT - (n + 1) * M) * D]).then_inc(emb_ready, 1)

            def product(L, t):
                if t == 0:
                    dve.wait_ge(first_in, 16 * SH * (L + 1))
                turns = (NPAIR - 1 - t % SLOTS) // SLOTS + 1
                dve.wait_ge(second_in[t % SLOTS], 16 * (L * turns + t // SLOTS + 1))
                if t >= PR:
                    dve.wait_ge(prodl_ready, L * NPAIR + t - PR + 1)
                elif not (isinstance(L, int) and L == 0):
                    dve.wait_ge(prodl_ready, L * NPAIR)
                dve.tensor_tensor(prod[:, t % PR, :], second[:, t % SLOTS, :], first[:], ALU.mult).then_inc(prod_ready, 1)

            def product_low(L, t):
                n = L * NPAIR + t
                dve.wait_ge(prodh_ready, n + 1)
                dve.tensor_tensor(prod_lo[:, t % HR, :], prod[:, t % PR, :], prod_hi[:, t % HR, :].bitcast(F32),
                                  ALU.subtract).then_inc(prodl_ready, 1)

            def x1_low(L, j0, j1):
                dve.wait_ge(x1h_ready, L * DG + j1)
                cs = slice(j0 * P, j1 * P)
                dve.tensor_tensor(x1_lo[:, cs], x1_sb[:, cs], x1_hi[:, cs].bitcast(F32),
                                  ALU.subtract).then_inc(x1l_ready, j1 - j0)

            def z0_sum(bt, g, dq):
                dve.wait_ge(x1_ready, g + 1)
                if dq == 0 and not (isinstance(bt, int) and bt == 0):
                    dve.wait_ge(z0_copied, bt)
                dve.tensor_reduce(z0_sb[:, dq * GB:(dq + 1) * GB].rearrange("h (k b) -> h k b", k=DG),
                                  x1_sb[:].rearrange("h (k d b) -> h k b d", k=DG, d=D),
                                  AX.X, ALU.add).then_inc(z0_ready, 1)

            def iteration(bt, more):
                for dq in range(GROUPS):
                    g = bt * GROUPS + dq
                    L = g + 1
                    ahead = more or dq < GROUPS - 1
                    dve.wait_ge(x0g_ready, g + 1)
                    for q in range(NQ):
                        if OWNER[q] == "V":
                            macs(g, dq, q)
                        if q == 2:
                            x1_low(g, DG - 1, DG)
                        if ahead and q in PROD_Q:
                            product(L, PROD_Q.index(q))
                        if ahead and q in LOW_Q:
                            product_low(L, LOW_Q.index(q))
                        if q % NB == REDUCE_Q and q > NB:
                            reduce_x2(g, dq * DG + q // NB - 1)
                        if q == REDUCE_Q and not (isinstance(g, int) and g == 0):
                            reduce_x2(g - 1, (dq * DG - 1) % NK)
                        if q == 30:
                            z0_sum(bt, g, dq)
                        if q == 36 and ahead:
                            x1_low(L, 0, DG - 1)
                        if more and dq == GROUPS - 2 and q == EXTEND_Q:
                            extend_embeddings(bt + 1)

            dve.memset(blocks[:], 0.0).then_inc(blocks_zeroed, 1)
            dve.wait_ge(small_in, 16 * 4)
            dve.tensor_tensor(pairs, pairs, pairs_b, ALU.add).then_inc(pairs_ready, 1)
            dve.wait_ge(blocks_zeroed, 1)
            dve.tensor_copy(blocks[:].rearrange("p a j w -> p (a j) w")[:, :, KB * M:GW],
                            mask[:].unsqueeze(1).to_broadcast([P, 2 * DG, KB])).then_inc(blocks_init, 1)
            dve.wait_ge(k1h_ready, 1)
            dve.tensor_tensor(k1_lo[:], k1_stage, k1_hi[:].bitcast(F32), ALU.subtract).then_inc(k1l_ready, 1)
            dve.wait_ge(halves_ready, 1)
            dve.tensor_tensor(pairs_lo[:], pairs, pairs_hi[:].bitcast(F32), ALU.subtract).then_inc(halves_ready, 1)
            extend_embeddings(0)
            product(0, 0)
            product(0, 1)
            for t in range(NPAIR):
                if t + 2 < NPAIR:
                    product(0, t + 2)
                product_low(0, t)
            x1_low(0, 0, DG - 1)
            iteration(0, True)
            with dve.Fori(1, BT - 1) as bt:
                iteration(bt, True)
            iteration(BT - 1, False)
            reduce_x2(BT * GROUPS - 1, NK - 1)

        @block.scalar
        def _(act):
            def scale_bank(g, dq, q):
                j, n, e = q // NB, q % NB, RANK[q]
                act.wait_ge(ys_full, g * NS + e + 1)
                first = e == S_AT[j]
                if first:
                    dst = sums[:, j, MB:2 * MB, :].rearrange("p s o -> p (s o)")
                    if not (isinstance(g, int) and g == 0):
                        act.wait_ge(x2_ready, (g - 1) * DG + j + 1)
                else:
                    add = ADD_AT[j] + e - S_AT[j] - 1
                    dst = scaled[:, add % SR, :]
                    if not (isinstance(g, int) and g == 0 and add < SR):
                        act.wait_ge(pool_added, g * NADD + add - SR + 1)
                for i in range(MB):
                    ins = act.activation(dst[:, i * H:(i + 1) * H], ps_y[q % YR][:, i * H:(i + 1) * H], ACT.Copy,
                                         scale=x0_g[:, dq * DG + j, n * MB + i:n * MB + i + 1])
                ins.then_inc(scaled_ready, 1)

            def x0_out(t, c, banks=(ps_s,)):
                act.wait_ge(x0_full, t * GROUPS + c + 1)
                if c == 0 and not (isinstance(t, int) and t == 0):
                    act.wait_ge(x0g_full, t * GROUPS)
                    act.wait_ge(prod_ready, t * GROUPS * NPAIR)
                n = D // GROUPS
                act.activation(x0t_v[:, c * n:(c + 1) * n], banks[c % len(banks)][:].rearrange("m (d k b) -> m d k b", d=n, k=NK),
                               ACT.Copy).then_inc(x0t_ready, 1)

            def x0g_out(g, t, dq):
                act.wait_ge(x0g_full, g + 1)
                if not (isinstance(g, int) and g < GROUPS):
                    act.wait_ge(mac_done, (g - GROUPS + 1) * NV * MB)
                    act.wait_ge(scaled_ready, (g - GROUPS + 1) * NS)
                    act.wait_ge(blocks_in[dq % 2], 16 * KB * ((t - 1) * (GROUPS // 2) + dq // 2 + 1))
                act.activation(x0_g[:, dq * DG:(dq + 1) * DG, :].rearrange("p k m -> p (k m)"), ps_tail[:, 0:DG * M],
                               ACT.Copy).then_inc(x0g_ready, 1)

            def product_high(L, t):
                n = L * NPAIR + t
                act.wait_ge(prod_ready, n + 1)
                if t < HR:
                    act.wait_ge(pair_mm, L * NPAIR)
                else:
                    act.wait_ge(pair_mm, n - HR + 1)
                act.activation(prod_hi[:, t % HR, :], prod[:, t % PR, :], ACT.Copy).then_inc(prodh_ready, 1)

            def x1_out(L):
                act.wait_ge(pair_mm, (L + 1) * NPAIR)
                act.wait_ge(z0_ready, L)
                act.wait_ge(x1l_ready, L * DG)
                act.activation(x1_sb[:], ps_x1[:], ACT.Copy).then_inc(x1_ready, 1)

            def x1_high(L, j0, j1):
                act.wait_ge(x1_ready, L + 1)
                if not (isinstance(L, int) and L == 0):
                    act.wait_ge(ys_full, (L - 1) * NS + S_AT[j1])
                cs = slice(j0 * P, j1 * P)
                act.activation(x1_hi[:, cs], x1_sb[:, cs], ACT.Copy).then_inc(x1h_ready, j1 - j0)

            def gram_out(t, k):
                act.wait_ge(gram_full, t * NK + k + 1)
                act.activation(gram[:, k, :], ps_tail[:, 0:GW], ACT.Copy).then_inc(gram_ready, 1)

            def z0_out(t):
                act.wait_ge(z0_ready, (t + 1) * GROUPS)
                if not (isinstance(t, int) and t == 0):
                    act.wait_ge(h1_full, t)
                act.activation(z0_mlp[:], z0_sb[:], ACT.Copy).then_inc(z0_copied, 1)

            def z1_out(t):
                act.wait_ge(gram_ready, (t + 1) * NK)
                act.activation(z1_sb[:].rearrange("h (k b) -> h k b", k=NK), gram[:, :, KB * M:GW],
                               ACT.Copy).then_inc(z1_ready, 1)

            def z2_out(t):
                act.wait_ge(z2_full, t + 1)
                act.activation(z2_sb[:], ps_tail[:, 0:P], ACT.Copy).then_inc(z2_ready, 1)

            def relu(t, full, ready, dst, bias, n, banks=None):
                act.wait_ge(full, t + 1)
                for o in range(n):
                    src = banks[o][:, 0:P] if banks else ps_tail[:, o * P:(o + 1) * P]
                    ins = act.activation(dst[:, o, :], src, ACT.Relu, bias=bias[:, o:o + 1])
                ins.then_inc(ready, 1)

            def y_out(t):
                act.wait_ge(y_full, t + 1)
                act.activation(y_sb[:], ps_tail[0:1, 0:P], ACT.Copy).then_inc(y_ready, 1)

            def iteration(bt, tail, more):
                for dq in range(GROUPS):
                    g = bt * GROUPS + dq
                    L = g + 1
                    ahead = more or dq < GROUPS - 1
                    act.wait_ge(x0g_ready, g + 1)
                    for q in range(NQ):
                        if OWNER[q] == "S":
                            scale_bank(g, dq, q)
                        if q == 1:
                            x1_high(g, DG - 1, DG)
                        if ahead and q in HIGH_Q:
                            product_high(L, HIGH_Q.index(q))
                        if ahead and q == X0_BLOCKS_Q[dq] + 2:
                            x0g_out(L, bt + (dq + 1) // GROUPS, (dq + 1) % GROUPS)
                        if q - 2 in GRAM_Q[dq]:
                            gram_out(bt, FIRST_K[dq] + GRAM_Q[dq].index(q - 2))
                        if dq == GROUPS - 1 and q == 34:
                            z0_out(bt)
                        if tail and dq == 0 and q == LAST_GRAM_Q + 2:
                            gram_out(bt - 1, NK - 1)
                            z1_out(bt - 1)
                        if tail and dq == 0 and q == LAYER2_Q + LAYER2_STEPS + 1:
                            z2_out(bt - 1)
                        if tail and dq == 1 and q == MLP1_Q[-1] + 2:
                            relu(bt - 1, h1_full, h1_ready, h1_sb, b1_sb, O1)
                        if tail and dq == 1 and q == MLP2_Q[-1] + 2:
                            relu(bt - 1, h2_full, h2_ready, h2_sb, b2_sb, O2)
                        if tail and dq == 1 and q == MLP3_Q + 2:
                            y_out(bt - 1)
                        if more and dq == GROUPS - 2 and q in X0_OUT_Q:
                            x0_out(bt + 1, X0_OUT_Q.index(q))
                        if q == 31 and ahead:
                            x1_out(L)
                            x1_high(L, 0, DG - 1)

            act.wait_ge(small_in, 16 * 4)
            act.wait_ge(pairs_ready, 1)
            act.activation(pairs_hi[:], pairs, ACT.Copy).then_inc(halves_ready, 1)
            act.wait_ge(k1_in, 16)
            act.activation(k1_hi[:], k1_stage, ACT.Copy).then_inc(k1h_ready, 1)
            for c in range(GROUPS):
                x0_out(0, c, ps_first)
            x0g_out(0, 0, 0)
            for t in range(NPAIR):
                product_high(0, t)
            x1_out(0)
            x1_high(0, 0, DG - 1)
            act.wait_ge(halves_ready, 2)
            act.wait_ge(late_in, 16 * 7)
            iteration(0, False, True)
            with act.Fori(1, BT - 1) as bt:
                iteration(bt, True, True)
            iteration(BT - 1, True, False)
            t = BT - 1
            gram_out(t, NK - 1)
            z1_out(t)
            z2_out(t)
            relu(t, h1_full, h1_ready, h1_sb, b1_sb, O1, ps_h1)
            relu(t, h2_full, h2_ready, h2_sb, b2_sb, O2)
            y_out(t)

        @block.gpsimd
        def _(pool):
            def gathers(t, f0, f1):
                for f in range(f0, f1):
                    pool.indirect_dma_start(emb[:, f * D:(f + 1) * D], None, tables[f],
                                            bass.IndirectOffsetOnAxis(ap=idx[:, f:f + 1], axis=0)).then_inc(gathered, 16)

            def load_idx(t):
                pool.wait_ge(gathered, t * M * 16)
                pool.nop(nofuse=True)
                pool.dma_start(idx[:], ids[bass.ds(t * P, P), :]).then_inc(idx_in, 16)

            def may_gather(t):
                pool.wait_ge(idx_in, 16 * (t + 1))
                pool.nop(nofuse=True)
                pool.wait_ge(x0_full, t * GROUPS)
                pool.nop(nofuse=True)

            def group(bt, dq, fetch):
                g = bt * GROUPS + dq
                far = dq == GROUPS - 1
                f0, f1 = GATHER_AT[(dq + 1) % GROUPS], GATHER_AT[(dq + 1) % GROUPS + 1]
                at = 0 if dq == GROUPS - 2 else 3
                if fetch and far:
                    load_idx(bt + 2)
                for j in range(DG):
                    dst = sums[:, j, MB:2 * MB, :].rearrange("p s o -> p (s o)")
                    for e in range(1, S_AT[j + 1] - S_AT[j]):
                        slot = ADD_AT[j] + e - 1
                        pool.wait_ge(scaled_ready, g * NS + S_AT[j] + e + 1)
                        if e > 1:
                            pool.wait_ge(pool_added, g * NADD + slot)
                        pool.tensor_tensor(dst, dst, scaled[:, slot % SR, :],
                                           ALU.add).then_inc(pool_added, 1)
                        if fetch and far and slot == 2:
                            may_gather(bt + 2)
                        f = f0 + slot - at
                        if fetch and f0 <= f < f1:
                            gathers(bt + 2 if far else bt + 1, f, f + 1)

            pool.dma_start(idx[:], ids[0:P, :]).then_inc(idx_in, 16)
            pool.wait_ge(idx_in, 16)
            gathers(0, 0, M - 5)
            pool.memset(warm_up_mark[:], 0.0).then_inc(gathers_near_end, 1)
            gathers(0, M - 5, M)
            load_idx(1)
            may_gather(1)
            gathers(1, 0, GATHER_AT[1])
            for dq in range(GROUPS - 1):
                group(0, dq, True)
            with pool.Fori(0, BT - 2) as bt:
                group(bt, GROUPS - 1, True)
                for dq in range(GROUPS - 1):
                    group(bt + 1, dq, True)
            group(BT - 2, GROUPS - 1, False)
            for dq in range(GROUPS):
                group(BT - 1, dq, False)


def kernel(**inputs):
    import numpy as np
    from concourse import bacc
    from concourse.bass_utils import run_bass_kernel_spmd

    a = {k: np.asarray(v) for k, v in inputs.items()}
    k0 = a["L0_rec_k0"]
    i, j = np.tile(np.arange(M), SH), np.repeat(np.arange(SH), M)
    h = (i - NPAIR * j) % M
    lay_a, lay_b = [], []
    for t in range(NPAIR):
        shift, m = NPAIR * j + t, (i + t) % M
        lay_a.append(k0[:, h, m].T)
        twice = np.isin(shift, (0, M // 2))
        lay_b.append(np.where(twice[:, None], np.zeros((), k0.dtype), k0[:, m, h].T))
    arrays = {
        "ids": a["ids"],
        "dense_t": np.ascontiguousarray(a["dense_ctx"].T),
        "k0a": np.ascontiguousarray(np.concatenate(lay_a, axis=1)),
        "k0b": np.ascontiguousarray(np.concatenate(lay_b, axis=1)),
        "k1": np.ascontiguousarray(a["L0_rec_k1"].transpose(1, 2, 0)).reshape(H, M * H),
        "k2": np.ascontiguousarray(a["L0_rec_k2"].transpose(1, 2, 0)).reshape(H, M * H),
        "w1": np.ascontiguousarray(a["W_top1"][:3 * P].reshape(3, P, F1).transpose(1, 0, 2)),
        "w1d": np.ascontiguousarray(a["W_top1"][3 * P:]),
        "b1": np.ascontiguousarray(a["b_top1"].reshape(O1, P).T),
        "w2": np.ascontiguousarray(a["W_top2"].reshape(O1, P, F2).transpose(1, 0, 2)),
        "b2": np.ascontiguousarray(a["b_top2"].reshape(O2, P).T),
        "w3": np.ascontiguousarray(a["W_top3"].reshape(O2, P).T),
        "ident_in": np.eye(P, dtype=np.float32),
        "mask_in": np.tile(np.eye(KB, dtype=np.float32), (D, 1)),
    }
    tables = {f"tbl_{f}": a[f"tbl_{f}"] for f in range(M)}
    nc = bacc.Bacc("TRN2", target_bir_lowering=False, num_devices=1)

    def dram(name, array):
        return nc.dram_tensor(name, array.shape, mybir.dt.from_np(array.dtype), kind="ExternalInput").ap()

    args = {name: dram(name, array) for name, array in arrays.items()}
    tabs = [dram(name, array) for name, array in tables.items()]
    out = nc.dram_tensor("out", [B, 1], F32, kind="ExternalOutput").ap()
    build(nc, tables=tabs, out=out, **args)
    r = run_bass_kernel_spmd(nc, [{**arrays, **tables}], core_ids=[0])
    return r.results[0]["out"]
```
